# Optimizing a Trainium2 kernel written in Bass

```python
import numpy as np
import jax
import jax.numpy as jnp

def _softmax(x, axis=-1):
    return jax.nn.softmax(x, axis=axis)

def _gelu(x):
    return jax.nn.gelu(x, approximate=True)

def _silu(x):
    return jax.nn.silu(x)

def _sigmoid(x):
    return jax.nn.sigmoid(x)

def _layernorm(x, axis=-1, eps=1e-05):
    m = jnp.mean(x, axis=axis, keepdims=True)
    v = jnp.var(x, axis=axis, keepdims=True)
    return (x - m) / jnp.sqrt(v + eps)

def _scatter_add(tgt, idx, src, axis=0):
    return tgt.at[idx].add(src)

def _segment_sum(src, seg, n):
    return jax.ops.segment_sum(src, seg, n)
kernel_name = 'mk_cond_resid_d4_seqx_r8_0b0ad2'

def setup_inputs(seed: int=0):
    np.random.seed(seed)
    _w = jnp.asarray

    def _rec_inputs():
        import jax
        import jax.numpy as jnp
        _rk = jax.random.key(seed)
        x = -0.000125 + 0.9999 * jax.random.normal(jax.random.fold_in(_rk, 1), (32, 32, 256), jnp.float32)
        _lenS = 32 - jax.random.randint(jax.random.fold_in(_rk, 7), (32,), 0, max(1, 32 // 4) + 1, jnp.int32)
        _lenS2 = 32 - jax.random.randint(jax.random.fold_in(_rk, 8), (32,), 0, max(1, 32 // 4) + 1, jnp.int32)
        itok_B_0_3 = jax.random.randint(jax.random.fold_in(_rk, 11), (32,), 0, 4, jnp.int32)
        itok_B_0_7 = jax.random.randint(jax.random.fold_in(_rk, 12), (32,), 0, 8, jnp.int32)
        itok_B_1_198 = jax.random.randint(jax.random.fold_in(_rk, 13), (32,), 1, 199, jnp.int32)
        itok_Bx257_0_4111 = jax.random.randint(jax.random.fold_in(_rk, 14), (32, 257), 0, 514, jnp.int32)
        itok_B_37_3939 = jax.random.randint(jax.random.fold_in(_rk, 15), (32,), 37, 3940, jnp.int32)
        return (x, itok_B_0_3, itok_B_0_7, itok_B_1_198, itok_Bx257_0_4111, itok_B_37_3939)
    x, itok_B_0_3, itok_B_0_7, itok_B_1_198, itok_Bx257_0_4111, itok_B_37_3939 = _rec_inputs()

    def _L0_cond_setup():
        import jax, jax.numpy as jnp
        import numpy as np
        B, S, D_IN, D_OUT, R, E = (8, 256, 256, 256, 16, 4)
        key = jax.random.key(seed)
        ks = jax.random.split(key, 7)
        x = jax.random.normal(ks[0], (B, S, D_IN), dtype=jnp.float32)
        W_base = jax.random.normal(ks[1], (D_OUT, D_IN), dtype=jnp.float32) * 0.02
        Wt = jax.random.normal(ks[2], (D_IN, D_IN), dtype=jnp.float32) * 0.02
        A = jax.random.normal(ks[3], (E, R, D_IN), dtype=jnp.float32) * 0.02
        B_w = jax.random.normal(ks[4], (E, D_OUT, R), dtype=jnp.float32) * 0.02
        Wp = jax.random.normal(ks[5], (D_OUT, D_OUT), dtype=jnp.float32) * 0.02
        scaling = jnp.ones((E,), dtype=jnp.float32)
        adapter_idx = jax.random.randint(ks[6], (B,), 0, E)
        return {'x': x, 'W_base': W_base, 'Wt': Wt, 'A': A, 'B_w': B_w, 'Wp': Wp, 'scaling': scaling, 'adapter_idx': adapter_idx}
    _L0_cond_all = _L0_cond_setup()
    _L0_cond_in = {k: v for k, v in _L0_cond_all.items() if k in ('W_base', 'Wt', 'A', 'B_w', 'Wp', 'scaling')}
    del _L0_cond_all

    def _L1_cond_setup():
        import jax, jax.numpy as jnp
        import numpy as np
        B, C, D, T, N_SUBJECTS = (128, 32, 32, 256, 8)
        key = jax.random.key(seed)
        kx, ks, kw = jax.random.split(key, 3)
        x = jax.random.normal(kx, (B, C, T), dtype=jnp.float32)
        subjects = jax.random.randint(ks, (B,), 0, N_SUBJECTS, dtype=jnp.int64)
        weights = jax.random.normal(kw, (N_SUBJECTS, C, D), dtype=jnp.float32) * (1.0 / C ** 0.5)
        return {'x': x, 'subjects': subjects, 'weights': weights}
    _L1_cond_all = _L1_cond_setup()
    _L1_cond_in = {k: v for k, v in _L1_cond_all.items() if k in ('weights',)}
    del _L1_cond_all

    def _L2_cond_setup():
        import jax, jax.numpy as jnp
        import numpy as np
        B, C, T = (128, 32, 256)
        S, D = (200, 32)
        key = jax.random.key(seed)
        k1, k2, k3 = jax.random.split(key, 3)
        x = jax.random.normal(k1, (B, C, T), dtype=jnp.float32)
        conditions = jax.random.randint(k2, (B,), 0, S, dtype=jnp.int64)
        weights = jax.random.normal(k3, (S, C, D), dtype=jnp.float32) / jnp.sqrt(jnp.float32(C))
        return {'x': x, 'conditions': conditions, 'weights': weights}
    _L2_cond_all = _L2_cond_setup()
    _L2_cond_in = {k: v for k, v in _L2_cond_all.items() if k in ('weights',)}
    del _L2_cond_all

    def _L3_cond_setup():
        import jax, jax.numpy as jnp
        import numpy as np
        H, G, HD = (8, 4, 32)
        GSZ = H // G
        BLOCK = 16
        WINDOW = 128
        SCALE = 256.0 ** (-0.5)
        EPS = 1e-06
        THETA = 10000.0
        B, T, D = (16, 4, 256)
        NBLK = 257

        def _rms(x, scale):
            var = jnp.mean(x * x, axis=-1, keepdims=True)
            return x * jax.lax.rsqrt(var + EPS) * (1.0 + scale)

        def _rope(x, pos):
            half = HD // 2
            inv = 1.0 / THETA ** (jnp.arange(half, dtype=jnp.float32) / half)
            ang = pos[:, :, None].astype(jnp.float32) * inv
            cos = jnp.cos(ang)[:, None, :, :]
            sin = jnp.sin(ang)[:, None, :, :]
            x1, x2 = (x[..., :half], x[..., half:])
            return jnp.concatenate([x1 * cos - x2 * sin, x2 * cos + x1 * sin], axis=-1)
        key = jax.random.key(seed)
        ks = jax.random.split(key, 10)
        inv_d = 1.0 / np.sqrt(D)
        return {'x': jax.random.normal(ks[0], (B, T, D), jnp.float32), 'Wq': jax.random.normal(ks[1], (H * HD, D), jnp.float32) * inv_d, 'Wk': jax.random.normal(ks[2], (G * HD, D), jnp.float32) * inv_d, 'Wv': jax.random.normal(ks[3], (G * HD, D), jnp.float32) * inv_d, 'Wo': jax.random.normal(ks[4], (D, H * HD), jnp.float32) * inv_d, 'q_norm_scale': jax.random.normal(ks[5], (HD,), jnp.float32) * 0.02, 'k_norm_scale': jax.random.normal(ks[6], (HD,), jnp.float32) * 0.02, 'k_blocks': jax.random.normal(ks[7], (B * NBLK, G, BLOCK, HD), jnp.float32), 'v_blocks': jax.random.normal(ks[8], (B * NBLK, G, BLOCK, HD), jnp.float32), 'block_tables': jnp.arange(B * NBLK, dtype=jnp.int32).reshape(B, NBLK), 'kv_lens': jax.random.randint(ks[9], (B,), 0, 512, dtype=jnp.int32)}
    _L3_cond_all = _L3_cond_setup()
    _L3_cond_in = {k: v for k, v in _L3_cond_all.items() if k in ('Wq', 'Wk', 'Wv', 'Wo', 'q_norm_scale', 'k_norm_scale', 'k_blocks', 'v_blocks')}
    del _L3_cond_all
    return {'x': x, 'itok_B_0_3': itok_B_0_3, 'itok_B_0_7': itok_B_0_7, 'itok_B_1_198': itok_B_1_198, 'itok_Bx257_0_4111': itok_Bx257_0_4111, 'itok_B_37_3939': itok_B_37_3939, 'L0_cond_W_base': _L0_cond_in['W_base'], 'L0_cond_Wt': _L0_cond_in['Wt'], 'L0_cond_A': _L0_cond_in['A'], 'L0_cond_B_w': _L0_cond_in['B_w'], 'L0_cond_Wp': _L0_cond_in['Wp'], 'L0_cond_scaling': _L0_cond_in['scaling'], 'L1_cond_weights': _L1_cond_in['weights'], 'L2_cond_weights': _L2_cond_in['weights'], 'L3_cond_Wq': _L3_cond_in['Wq'], 'L3_cond_Wk': _L3_cond_in['Wk'], 'L3_cond_Wv': _L3_cond_in['Wv'], 'L3_cond_Wo': _L3_cond_in['Wo'], 'L3_cond_q_norm_scale': _L3_cond_in['q_norm_scale'], 'L3_cond_k_norm_scale': _L3_cond_in['k_norm_scale'], 'L3_cond_k_blocks': _L3_cond_in['k_blocks'], 'L3_cond_v_blocks': _L3_cond_in['v_blocks']}

def reference(x, itok_B_0_3, itok_B_0_7, itok_B_1_198, itok_Bx257_0_4111, itok_B_37_3939, L0_cond_W_base, L0_cond_Wt, L0_cond_A, L0_cond_B_w, L0_cond_Wp, L0_cond_scaling, L1_cond_weights, L2_cond_weights, L3_cond_Wq, L3_cond_Wk, L3_cond_Wv, L3_cond_Wo, L3_cond_q_norm_scale, L3_cond_k_norm_scale, L3_cond_k_blocks, L3_cond_v_blocks):
    import jax
    import jax.numpy as jnp

    def _L0_cond_ref(x, W_base, Wt, A, B_w, Wp, scaling, adapter_idx):
        import jax, jax.numpy as jnp
        import numpy as np
        B, S, D_IN, D_OUT, R, E = (8, 256, 256, 256, 16, 4)
        base = jnp.einsum('bsi,oi->bso', x, W_base)
        h = jnp.einsum('bsi,ji->bsj', x, Wt)
        Ab = A[adapter_idx]
        Bb = B_w[adapter_idx]
        sc = scaling[adapter_idx]
        z = jnp.einsum('bsj,brj->bsr', h, Ab)
        l = jnp.einsum('bsr,bor->bso', z, Bb)
        lora_out = jnp.einsum('bso,po->bsp', l, Wp) * sc[:, None, None]
        return base + lora_out

    def _L1_cond_ref(x, subjects, weights):
        import jax, jax.numpy as jnp
        import numpy as np
        B, C, D, T, N_SUBJECTS = (128, 32, 32, 256, 8)
        w = weights[subjects]
        out = jnp.einsum('bct,bcd->bdt', x, w)
        return out

    def _L2_cond_ref(x, conditions, weights):
        import jax, jax.numpy as jnp
        import numpy as np
        B, C, T = (128, 32, 256)
        S, D = (200, 32)
        w = weights[conditions]
        return jnp.einsum('bct,bcd->bdt', x, w)

    def _L3_cond_ref(x, Wq, Wk, Wv, Wo, q_norm_scale, k_norm_scale, k_blocks, v_blocks, block_tables, kv_lens):
        import jax, jax.numpy as jnp
        import numpy as np
        H, G, HD = (8, 4, 32)
        GSZ = H // G
        BLOCK = 16
        WINDOW = 128
        SCALE = 256.0 ** (-0.5)
        EPS = 1e-06
        THETA = 10000.0
        B, T, D = (16, 4, 256)
        NBLK = 257

        def _rms(x, scale):
            var = jnp.mean(x * x, axis=-1, keepdims=True)
            return x * jax.lax.rsqrt(var + EPS) * (1.0 + scale)

        def _rope(x, pos):
            half = HD // 2
            inv = 1.0 / THETA ** (jnp.arange(half, dtype=jnp.float32) / half)
            ang = pos[:, :, None].astype(jnp.float32) * inv
            cos = jnp.cos(ang)[:, None, :, :]
            sin = jnp.sin(ang)[:, None, :, :]
            x1, x2 = (x[..., :half], x[..., half:])
            return jnp.concatenate([x1 * cos - x2 * sin, x2 * cos + x1 * sin], axis=-1)
        Bx, Tx, _ = x.shape
        q = jnp.einsum('btd,od->bto', x, Wq).reshape(Bx, Tx, H, HD).transpose(0, 2, 1, 3)
        k = jnp.einsum('btd,od->bto', x, Wk).reshape(Bx, Tx, G, HD).transpose(0, 2, 1, 3)
        v = jnp.einsum('btd,od->bto', x, Wv).reshape(Bx, Tx, G, HD).transpose(0, 2, 1, 3)
        q = _rms(q, q_norm_scale)
        k = _rms(k, k_norm_scale)
        pos = kv_lens[:, None] + jnp.arange(Tx, dtype=jnp.int32)
        q = _rope(q, pos)
        k = _rope(k, pos)
        slot = pos // BLOCK
        off = pos % BLOCK
        blk = jnp.take_along_axis(block_tables, slot, axis=1)
        k_blocks = k_blocks.at[blk, :, off, :].set(k.transpose(0, 2, 1, 3))
        v_blocks = v_blocks.at[blk, :, off, :].set(v.transpose(0, 2, 1, 3))
        k_all = k_blocks[block_tables].transpose(0, 2, 1, 3, 4).reshape(Bx, G, -1, HD)
        v_all = v_blocks[block_tables].transpose(0, 2, 1, 3, 4).reshape(Bx, G, -1, HD)
        S = k_all.shape[2]
        qg = q.reshape(Bx, G, GSZ, Tx, HD)
        scores = jnp.einsum('bghtd,bgsd->bghts', qg, k_all) * SCALE
        kpos = jnp.arange(S, dtype=jnp.int32)
        allowed = (kpos[None, None, :] <= pos[:, :, None]) & (kpos[None, None, :] > pos[:, :, None] - WINDOW)
        scores = jnp.where(allowed[:, None, None, :, :], scores, -jnp.inf)
        p = jax.nn.softmax(scores, axis=-1)
        o = jnp.einsum('bghts,bgsd->bghtd', p, v_all).reshape(Bx, H, Tx, HD)
        o = o.transpose(0, 2, 1, 3).reshape(Bx, Tx, H * HD)
        return jnp.einsum('bto,do->btd', o, Wo)
    x = x + _L0_cond_ref(x, L0_cond_W_base, L0_cond_Wt, L0_cond_A, L0_cond_B_w, L0_cond_Wp, L0_cond_scaling, itok_B_0_3)
    x = x + _L1_cond_ref(x, itok_B_0_7, L1_cond_weights)
    x = x + _L2_cond_ref(x, itok_B_1_198, L2_cond_weights)
    x = x + _L3_cond_ref(x, L3_cond_Wq, L3_cond_Wk, L3_cond_Wv, L3_cond_Wo, L3_cond_q_norm_scale, L3_cond_k_norm_scale, L3_cond_k_blocks, L3_cond_v_blocks, itok_Bx257_0_4111, itok_B_37_3939)
    return x

_drawn_inputs = setup_inputs


def setup_inputs(seed=0):
    import zlib

    import numpy as np

    out = dict(_drawn_inputs(seed))
    spreads = {'L0_cond_scaling': (1.0, 0.6)}
    factors = {'L0_cond_Wt': 8.0,
     'L0_cond_A': 8.0,
     'L0_cond_B_w': 8.0,
     'L0_cond_Wp': 8.0,
     'L3_cond_Wk': 13.059,
     'L3_cond_q_norm_scale': 64.0,
     'L3_cond_k_norm_scale': 64.0,
     'L3_cond_k_blocks': 28.246,
     'L0_cond_W_base': 2.868,
     'L3_cond_Wq': 3.862,
     'L3_cond_v_blocks': 8.0}
    for name, (base, spread) in spreads.items():
        noise = np.random.default_rng([zlib.crc32(name.encode()), seed]).standard_normal(out[name].shape)
        drawn = base * np.exp(spread * noise) if base else spread * noise
        out[name] = jnp.asarray(drawn.astype(out[name].dtype))
    for name, factor in factors.items():
        out[name] = (out[name] * factor).astype(out[name].dtype)
    return out
```

```python
from contextlib import ExitStack

import concourse.bass as bass
import numpy as np
from concourse import mybir

ALU = mybir.AluOpType
ACT = mybir.ActivationFunctionType
F32 = mybir.dt.float32
BF16 = mybir.dt.bfloat16
I32 = mybir.dt.int32
U32 = mybir.dt.uint32
U16 = mybir.dt.uint16
AX_X = mybir.AxisListType.X

B, T, D = 32, 32, 256
P = 128
BT = P // T
TILES = B // BT
TOK = B * T
C = D // P
E, R = 4, 16
ER = E * R
G, HH, HD = 4, 2, 32
HALF = HD // 2
KW = G * HD
QW = HH * KW
HEADS = G * HH + G
WINDOW = 128
BLOCK = 16
SLOTS = 257
LOOK = 12
BACK = WINDOW // BLOCK
RUNS = 3
NCOL = B + TILES
KEYS = WINDOW + T
EPS = 1e-6
SCALE = float(D) ** -0.5
MASKED = -1e30
BIAS = float(1 << 17)
NONE = float(1 << 20)
MAGIC = 12582912.0
TWO_PI = (6.28125, 0.0019350051879882812, 3.019916050561552e-07)
PI_SAFE = 3.1415925
AHEAD = 6

CONST = {}
_at = 0
for _name, _n in (("ident", P), ("slot", SLOTS), ("look", LOOK), ("target", 3), ("offset", NCOL),
                  ("t", 1), ("inv", HALF), ("same", P), ("pick", 4 * TILES), ("adapter", 1),
                  ("order", RUNS * B), ("key", WINDOW), ("group", P), ("t_eye", T),
                  ("q_scale", HD), ("k_scale", HD), ("scaling", 1)):
    CONST[_name] = (_at, _n)
    _at += _n
CONST_W = _at

INTS = {"lens_col": (0, NCOL), "lens_rb": (NCOL, 1), "w1_idx": (NCOL + 1, 1), "w2_idx": (NCOL + 2, 1),
        "adapter_idx": (NCOL + 3, B), "table": (NCOL + 3 + B, SLOTS)}
INTS_W = NCOL + 3 + B + SLOTS
LOW = {"Wt": (0, D), "AT": (C * D, ER), "Bo": (C * (D + ER), ER), "WpT": (C * (D + 2 * ER), D)}
LOW_W = C * (2 * D + 2 * ER)


def constants():
    p = np.arange(P)
    c = np.zeros((P, CONST_W), np.float32)

    def put(name, v):
        a, n = CONST[name]
        c[:, a:a + n] = v

    put("ident", np.eye(P))
    put("slot", np.arange(SLOTS)[None])
    put("look", np.arange(LOOK)[None])
    put("target", (p // B)[:, None] + 4 * np.arange(3)[None] - BACK)
    put("offset", np.concatenate([np.repeat(p[:, None], B, 1), np.repeat(WINDOW + p[:, None] % T, TILES, 1)], 1))
    put("t", (p % T)[:, None])
    put("inv", (np.float32(1.0) / np.float32(10000.0) ** (np.arange(HALF, dtype=np.float32) / np.float32(HALF)))[None])
    put("same", ((p[:, None] % B) % BT == p[None] // T))
    rb = np.arange(4 * TILES)
    put("pick", (p[:, None] // B == rb[None] // TILES) & ((p[:, None] % B) // BT == rb[None] % TILES))
    put("adapter", (p // R)[:, None])
    i, b = np.arange(RUNS * B) // B, np.arange(RUNS * B) % B
    put("order", (T * b + BLOCK * i)[None] + BIAS)
    put("key", np.arange(WINDOW)[None])
    put("group", p[:, None] // HD == p[None] // HD)
    put("t_eye", p[:, None] % T == np.arange(T)[None])
    return c


def mask_constants():
    t, key = np.arange(T)[:, None], np.arange(KEYS)[None]
    band = np.where((key > t) & (key <= t + WINDOW), 0.0, MASKED)
    sel = np.zeros((2, 32, B, G, T))
    sel[0] = np.eye(T)[:, None, None, :]
    sel[1] = np.eye(B)[:, :, None, None]
    return [(v.astype(np.float32).view(np.uint32) >> 16).astype(np.uint16) for v in (band, sel.reshape(64, B * P))]


def free(ap, *dims):
    return bass.AP(tensor=ap.tensor, offset=ap.offset, ap=[list(ap.ap[0])] + [list(d) for d in dims])


def dram(ap, *dims):
    return bass.AP(tensor=ap.tensor, offset=ap.offset, ap=[list(d) for d in dims])


def cond_resid_kernel(nc, ints, const, low, xT, WbT, W1T, W2, WqkvT, WoT, cache, band, select,
                      new_rows, w1_rows, w2_rows, out):
    with ExitStack() as ctx:
        def sb(name, shape, dt=F32):
            return ctx.enter_context(nc.sbuf_tensor(name, shape, dt))

        def sem(name):
            return ctx.enter_context(nc.semaphore(name))

        bank = [ctx.enter_context(nc.psum_tensor(f"bank{i}", [P, 512], F32)) for i in range(8)]

        cst = sb("cst", [P, CONST_W])
        ints_sb = sb("ints_sb", [P, INTS_W], I32)
        low_sb = sb("low_sb", [P, LOW_W])
        lens_dyn = sb("lens_dyn", [64, 1])
        xT_sb = sb("xT_sb", [P, C, TOK])
        Wb_sb = sb("Wb_sb", [P, C, D])
        Wqkv_sb = sb("Wqkv_sb", [P, C, QW + 2 * KW])
        Wo_sb = sb("Wo_sb", [P, HH, D])
        maskr = sb("maskr", [P, KEYS], BF16)
        sel_sb = sb("sel_sb", [P, B, P], BF16)

        slot0 = sb("slot0", [P, 1], I32)
        target = sb("target", [P, 3])
        junk = sb("junk", [P, 3, SLOTS])
        looked = sb("looked", [P, 3])
        look_all = sb("look_all", [P, 3, P])
        look_own = sb("look_own", [P, 3, 4 * TILES])
        ones = sb("ones", [P, P])
        eps = sb("eps", [P, 1])
        inblk = sb("inblk", [P, NCOL], I32)
        place = sb("place", [P, NCOL], I32)
        slot_of = sb("slot_of", [P, NCOL], I32)
        off_of = sb("off_of", [P, NCOL], I32)
        hit = sb("hit", [P, LOOK, NCOL])
        block_of = sb("block_of", [P, NCOL])
        row_of = sb("row_of", [P, NCOL])
        hist_idx = sb("hist_idx", [P, B], I32)
        run_lo = sb("run_lo", [P, RUNS, B])
        run_hi = sb("run_hi", [P, RUNS, B])
        run_shift = sb("run_shift", [P, RUNS, B])
        above = sb("above", [P, 8, RUNS * B])
        match = sb("match", [P, 8, RUNS * B])
        best = sb("best", [P, NCOL])
        nobody = sb("nobody", [P, NCOL])
        patch_idx = sb("patch_idx", [P, NCOL], I32)

        pos = sb("pos", [P, TILES])
        ang = sb("ang", [P, TILES, 2, HALF])
        turns = sb("turns", [P, TILES, 2, HALF])
        cossin = sb("cossin", [P, TILES, 2, HALF])
        plus1 = sb("plus1", [P, 2, HD])
        cross1 = sb("cross1", [P, 2, HD])
        rot_same = sb("rot_same", [P, TILES, 2, HD])
        rot_cross = sb("rot_cross", [P, TILES, 2, HD])

        mask0 = sb("mask0", [ER, B])
        AW_sb = sb("AW_sb", [P, C, ER])
        C_sb = sb("C_sb", [ER, D])
        zm = sb("zm", [ER, TOK])
        w1_sb = sb("w1_sb", [B, T * T])
        w2_sb = sb("w2_sb", [B, T * T])
        bd1 = sb("bd1", [P, TILES, P])
        bd2 = sb("bd2", [P, TILES, P])
        M_sb = sb("M_sb", [P, TILES, P])
        x1 = sb("x1", [P, TILES, D])
        x3T = sb("x3T", [P, TILES, C, P])

        qkv = sb("qkv", [P, TILES, QW + 2 * KW])
        sq = sb("sq", [P, 4, QW])
        ssum = sb("ssum", [P, TILES, HEADS])
        root = sb("root", [P, TILES, HEADS])
        rnorm = sb("rnorm", [P, TILES, HEADS])
        kn = sb("kn", [P, 2, G, HD])
        ks_ = sb("ks_", [P, 2, G, HD])
        kc = sb("kc", [P, 2, G, HD])
        qn = sb("qn", [P, HH * G, HD])
        qs_ = sb("qs_", [P, HH * G, HD])
        qc = sb("qc", [P, HH * G, HD])
        hist = sb("hist", [P, B, 2 * KW])
        KT = sb("KT", [P, 2, BT, KEYS])
        qbd = sb("qbd", [P, 2, HH * BT, G, T])
        Vbd = sb("Vbd", [P, 2, BT, KW])
        negmax = sb("negmax", [P, 4, HH])
        esum = sb("esum", [P, 2, BT * HH])
        rsum = sb("rsum", [P, BT * HH])
        rdiag = sb("rdiag", [P, 2, BT * HH, T])
        Pr = sb("Pr", [P, 8, HH, KEYS])
        PT = sb("PT", [P, 8, HH, P])
        PTn = sb("PTn", [P, 2, 2 * HH * P])
        oT = sb("oT", [P, 2, HH, BT, T])
        res = sb("res", [P, 2, D])

        def cv(name, rows=slice(0, P)):
            a, n = CONST[name]
            return cst[rows, a:a + n]

        def iv(name, rows=slice(0, P)):
            a, n = INTS[name]
            return ints_sb[rows, a:a + n]

        def lv(name):
            a, n = LOW[name]
            return low_sb[:, a:a + C * n].rearrange("p (c n) -> p c n", c=C)

        s_int, s_cst, s_low, s_x, s_wb, s_qkvw, s_wo, s_mask = map(sem, (
            "s_int", "s_cst", "s_low", "s_x", "s_wb", "s_qkvw", "s_wo", "s_mask"))
        s_w1g, s_w2g, s_w1d, s_w2d, s_bd1, s_bd2 = map(sem, ("s_w1g", "s_w2g", "s_w1d", "s_w2d", "s_bd1", "s_bd2"))
        s_new = sem("s_new")
        s_hist = [sem(f"s_hist{g}") for g in range(TILES)]
        s_patch = [sem(f"s_patch{g}") for g in range(TILES)]
        s_out = [sem(f"s_out{g}") for g in range(2)]
        z_bd, z_misc = sem("z_bd"), sem("z_misc")
        v_chain = sem("v_chain")
        v_look, v_idx, v_patch, v_wb, v_zm, v_B2, v_M, v_ang, v_dyn = map(sem, (
            "v_look", "v_idx", "v_patch", "v_wb", "v_zm", "v_B2", "v_M", "v_ang", "v_dyn"))
        v_ksum, v_k, v_qsum, v_q, v_max, v_kn, v_qbd, v_vbd, v_rdiag, v_o = map(sem, (
            "v_ksum", "v_k", "v_qsum", "v_q", "v_max", "v_kn", "v_qbd", "v_vbd", "v_rdiag", "v_o"))
        a_AW, a_C, a_x1, a_x3T, a_kv, a_ksq, a_kroot, a_qraw, a_qsq, a_qroot, a_sin = map(sem, (
            "a_AW", "a_C", "a_x1", "a_x3T", "a_kv", "a_ksq", "a_kroot", "a_qraw", "a_qsq", "a_qroot", "a_sin"))
        a_exp, a_kt, a_pt, a_ptn, a_res = map(sem, ("a_exp", "a_kt", "a_pt", "a_ptn", "a_res"))
        p_look, p_AW, p_C, p_z, p_x1, p_M, p_x3T, p_kv, p_qraw = map(sem, (
            "p_look", "p_AW", "p_C", "p_z", "p_x1", "p_M", "p_x3T", "p_kv", "p_qraw"))
        p_kt, p_kq, p_s, p_pt, p_ptn, p_o, p_res = map(sem, ("p_kt", "p_kq", "p_s", "p_pt", "p_ptn", "p_o", "p_res"))

        looked_ps = bank[0][:, 0:LOOK * NCOL].rearrange("p (j n) -> p j n", j=LOOK)
        AW_ps = bank[1][:, 0:C * ER].rearrange("p (c n) -> p c n", c=C)
        C_ps = bank[2][0:ER, 0:D]
        z_ps = [bank[3], bank[4]]
        x1_ps = [bank[5][:, 0:D], bank[6][:, 0:D], bank[7][:, 0:D]]
        M_ps = [bank[1][:, :].rearrange("p (i n) -> p i n", i=4), bank[2][:, :].rearrange("p (i n) -> p i n", i=4)]
        x3T_ps = [bank[3][:, 0:D].rearrange("p (c n) -> p c n", c=C), bank[4][:, 0:D].rearrange("p (c n) -> p c n", c=C)]
        kv_ps = [bank[i][:, 0:2 * KW] for i in (5, 6, 7)]
        q_ps = [bank[i][:, 0:QW] for i in (0, 1, 2)]

        S_ps = [bank[i][:, 0:HH * KEYS].rearrange("p (h k) -> p h k", h=HH) for i in (0, 1)]
        KT_ps = bank[2][:, :].rearrange("p (b k) -> p b k", b=BT)
        PT_ps = [bank[i][:, 0:HH * P].rearrange("p (h k) -> p h k", h=HH) for i in (3, 4)]
        KTn_ps = bank[5][:, 0:P]
        qT_ps = bank[5][:, P:P + HH * P].rearrange("p (h k) -> p h k", h=HH)
        PTn_ps = bank[5][:, 0:HH * P].rearrange("p (h k) -> p h k", h=HH)
        rsum_ps = bank[5][:, HH * P:2 * HH * P]
        O_ps = bank[6][:, 0:BT * HH * T].rearrange("p (b h t) -> p b h t", b=BT, h=HH)
        res_ps = bank[7][:, 0:D]

        block = ctx.enter_context(nc.Block())

        PATCHED = 16 * (BT + 1)

        @block.sync
        def _(sp):
            sp.dma_start(ints_sb[:], ints).then_inc(s_int, 16)
            sp.dma_start(low_sb[:], low).then_inc(s_low, 16)
            sp.dma_start(Wb_sb[:], WbT.rearrange("p (c n) -> p c n", c=C)).then_inc(s_wb, 16)
            for got, gathered, rows, wrote in ((s_w1g, w1_sb, w1_rows, s_w1d), (s_w2g, w2_sb, w2_rows, s_w2d)):
                sp.wait_ge(got, 16)
                sp.dma_start(rows, gathered[:]).then_inc(wrote, 16)
            sp.wait_ge(z_bd, 2)
            for rows, wrote, bd, done in ((w2_rows, s_w2d, bd2, s_bd2), (w1_rows, s_w1d, bd1, s_bd1)):
                sp.wait_ge(wrote, 16)
                for j in range(BT):
                    src = rows.rearrange("(n j) (k c) -> j k n c", j=BT, k=T)[j]
                    sp.dma_start(bd[T * j:T * j + T, :, T * j:T * j + T], src).then_inc(done, 16)
            sp.dma_start(Wo_sb[:], WoT.rearrange("p (h n) -> p h n", h=HH)).then_inc(s_wo, 16)
            new_tiles = new_rows.rearrange("(i p) n -> p i n", p=P)
            for j in range(TILES // 2):
                sp.wait_ge(v_k, j + 1)
                sp.wait_ge(a_kv, 2 * j + 2)
                sp.dma_start(new_tiles[:, 2 * j:2 * j + 2, :], qkv[:, 2 * j:2 * j + 2, QW:]).then_inc(s_new, 16)
            for i in range(TILES):
                sp.wait_ge(a_res, i + 1)
                sp.dma_start(out[P * i:P * i + P, :], res[:, i % 2, :]).then_inc(s_out[i % 2], 16)
            sp.wait_ge(s_out[0], 16 * (TILES // 2))
            sp.wait_ge(s_out[1], 16 * (TILES // 2))

        @block.gpsimd
        def _(pool):
            nc.gpsimd.memset(bd1[:], 0.0).then_inc(z_bd, 1)
            nc.gpsimd.memset(bd2[:], 0.0).then_inc(z_bd, 1)
            pool.wait_ge(s_int, 16)
            for rows, table, name, got in ((w1_sb, W1T, "w1_idx", s_w1g), (w2_sb, W2, "w2_idx", s_w2g)):
                nc.gpsimd.indirect_dma_start(
                    rows[:], None, table,
                    bass.IndirectOffsetOnAxis(ap=iv(name, slice(0, B)).bitcast(U32), axis=0)).then_inc(got, 16)

            def gather(i):
                for b in range(BT * i, BT * i + BT):
                    nc.gpsimd.indirect_dma_start(
                        hist[:, b, :], None, cache,
                        bass.IndirectOffsetOnAxis(ap=hist_idx[:, b:b + 1].bitcast(U32), axis=0)).then_inc(s_hist[i], 16)

            def patch(i):
                nc.gpsimd.indirect_dma_start(
                    qkv[:, i, QW:], None, new_rows,
                    bass.IndirectOffsetOnAxis(ap=patch_idx[:, B + i:B + i + 1].bitcast(U32), axis=0),
                    bounds_check=TOK - 1, oob_is_err=False).then_inc(s_patch[i], 16)
                pool.wait_ge(s_hist[i], 16 * BT)
                for b in range(BT * i, BT * i + BT):
                    nc.gpsimd.indirect_dma_start(
                        hist[:, b, :], None, new_rows,
                        bass.IndirectOffsetOnAxis(ap=patch_idx[:, b:b + 1].bitcast(U32), axis=0),
                        bounds_check=TOK - 1, oob_is_err=False).then_inc(s_patch[i], 16)

            pool.wait_ge(v_idx, 1)
            for i in range(AHEAD):
                gather(i)
            pool.wait_ge(z_bd, 2)
            nc.gpsimd.memset(sel_sb[64:P, :, :].bitcast(F32), 0.0).then_inc(z_misc, 1)
            pool.wait_ge(z_misc, 1)
            nc.gpsimd.memset(maskr[:].bitcast(F32), 0.0).then_inc(z_misc, 1)
            nc.gpsimd.memset(qbd[:], 0.0).then_inc(z_misc, 1)
            nc.gpsimd.memset(Vbd[:], 0.0).then_inc(z_misc, 1)
            pool.wait_ge(v_patch, 1)
            pool.wait_ge(s_new, 16 * (TILES // 2))
            for i in range(TILES):
                patch(i)
                if AHEAD + i < TILES:
                    gather(AHEAD + i)

        @block.scalar
        def _(act):
            act.dma_start(cst[:], const).then_inc(s_cst, 16)
            act.dma_start(xT_sb[:], xT.rearrange("p (c n) -> p c n", c=C)).then_inc(s_x, 16)
            act.dma_start(Wqkv_sb[:], WqkvT.rearrange("p (c n) -> p c n", c=C)).then_inc(s_qkvw, 16)

            act.wait_ge(p_AW, 1)
            nc.scalar.copy(AW_sb[:], AW_ps).then_inc(a_AW, 1)
            act.wait_ge(p_C, 1)
            nc.scalar.copy(C_sb[:], C_ps).then_inc(a_C, 1)
            for i in range(TILES):
                act.wait_ge(p_x1, i + 1)
                nc.scalar.copy(x1[:, i, :], x1_ps[i % 3]).then_inc(a_x1, 1)
            act.wait_ge(v_ang, 1)
            nc.scalar.activation(cossin[:], ang[:], ACT.Sin).then_inc(a_sin, 1)

            for i in range(TILES + 1):
                if i < TILES:
                    act.wait_ge(p_x3T, i + 1)
                    nc.scalar.copy(x3T[:, i, :, :], x3T_ps[i % 2]).then_inc(a_x3T, 1)
                if i >= 1:
                    j = i - 1
                    act.wait_ge(p_kv, i)
                    nc.scalar.copy(qkv[:, j, QW:], kv_ps[j % 3]).then_inc(a_kv, 1)
                    if j >= 4 and j % 2 == 0:
                        act.wait_ge(v_ksum, j // 2 - 1)
                    act.wait_ge(a_kv, i)
                    nc.scalar.activation(sq[:, j % 4, 0:KW], qkv[:, j, QW:QW + KW], ACT.Square).then_inc(a_ksq, 1)
                    if j % 2 == 1:
                        act.wait_ge(v_ksum, (j + 1) // 2)
                        nc.scalar.activation(root[:, j - 1:j + 1, HH * G:HEADS], ssum[:, j - 1:j + 1, HH * G:HEADS],
                                             ACT.Sqrt, scale=1.0 / HD, bias=eps[:, 0:1]).then_inc(a_kroot, 1)
            act.wait_ge(z_misc, 4)
            act.dma_start(sel_sb[0:64, :, :].bitcast(U16), select.rearrange("p (b n) -> p b n", b=B)).then_inc(s_mask, 16)
            act.dma_start(maskr[0:T, :].bitcast(U16), band).then_inc(s_mask, 16)
            for j in range(TILES):
                act.wait_ge(p_qraw, j + 1)
                nc.scalar.copy(qkv[:, j, 0:QW], q_ps[j % 3]).then_inc(a_qraw, 1)
                if j >= 4 and j % 2 == 0:
                    act.wait_ge(v_qsum, j // 2 - 1)
                elif j == 0:
                    act.wait_ge(v_ksum, TILES // 2)
                act.wait_ge(a_qraw, j + 1)
                nc.scalar.activation(sq[:, j % 4, :], qkv[:, j, 0:QW], ACT.Square).then_inc(a_qsq, 1)
            act.wait_ge(v_qsum, TILES // 2)
            nc.scalar.activation(root[:, :, 0:HH * G], ssum[:, :, 0:HH * G], ACT.Sqrt, scale=1.0 / HD,
                                 bias=eps[:, 0:1]).then_inc(a_qroot, 1)

            def kt_out(g):
                act.wait_ge(p_kt, g + 1)
                if g >= 2:
                    act.wait_ge(p_s, BT * (g - 1))
                nc.scalar.copy(KT[:, g % 2, :, 0:WINDOW], KT_ps).then_inc(a_kt, 1)

            def exps(n):
                g, j = divmod(n, BT)
                act.wait_ge(v_max, n + 1)
                if n >= 8:
                    act.wait_ge(p_pt, n - 7)
                    act.wait_ge(p_ptn, g - 1)
                    act.wait_ge(v_rdiag, g - 1)
                for h in range(HH):
                    nc.scalar.activation(Pr[:, n % 8, h, :], S_ps[n % 2][:, h, :], ACT.Exp, bias=negmax[:, n % 4, h:h + 1],
                                         accum_out=esum[:, g % 2, HH * j + h:HH * j + h + 1]).then_inc(a_exp, 1)

            def pt_out(n):
                act.wait_ge(p_pt, n + 1)
                if n >= 8:
                    act.wait_ge(p_o, n - 7)
                nc.scalar.copy(PT[:, n % 8, :, :], PT_ps[n % 2]).then_inc(a_pt, 1)

            def ptn_out(g):
                act.wait_ge(p_ptn, g + 1)
                if g >= 2:
                    act.wait_ge(p_o, BT * (g - 1))
                    act.wait_ge(v_o, g - 1)
                nc.scalar.copy(PTn[:, g % 2, :], bank[5][:, :]).then_inc(a_ptn, 1)

            def res_out(g):
                act.wait_ge(p_res, g + 1)
                if g >= 2:
                    act.wait_ge(s_out[g % 2], 16 * (g // 2))
                nc.scalar.copy(res[:, g % 2, :], res_ps).then_inc(a_res, 1)

            kt_out(0)
            for n in range(B + 7):
                g, k = divmod(n, BT)
                if n < B:
                    exps(n)
                if 2 <= n < B + 2:
                    pt_out(n - 2)
                if k == 1 and 1 <= g <= TILES:
                    ptn_out(g - 1)
                if k == 2:
                    if g + 1 < TILES:
                        kt_out(g + 1)
                    if n >= 10:
                        res_out((n - 10) // BT)

        @block.vector
        def _(dve):
            count = [0]

            def link(ins):
                count[0] += 1
                ins.then_inc(v_chain, 1)
                dve.wait_ge(v_chain, count[0])

            nc.vector.memset(eps[:], EPS)
            link(nc.vector.memset(ones[:], 1.0))
            dve.wait_ge(s_int, 16)
            link(nc.vector.tensor_single_scalar(slot0[:], iv("lens_rb"), 4, ALU.arith_shift_right))
            dve.wait_ge(s_cst, 16)
            link(nc.vector.tensor_scalar(target[:], cv("target"), slot0[:, 0:1], None, ALU.add))
            for m in range(3):
                last = nc.vector.scalar_tensor_tensor(out=junk[:, m, :], in0=cv("slot"), scalar=target[:, m:m + 1],
                                                      in1=iv("table"), op0=ALU.is_equal, op1=ALU.mult,
                                                      accum_out=looked[:, m:m + 1])
            link(last)
            nc.vector.tensor_tensor(look_all[:], free(cv("ident"), (0, 3), (1, P)), free(looked[:], (1, 3), (0, P)),
                                    ALU.mult).then_inc(v_look, 1)
            nc.vector.tensor_tensor(look_own[:], free(cv("pick"), (0, 3), (1, 4 * TILES)),
                                    free(looked[:], (1, 3), (0, 4 * TILES)), ALU.mult).then_inc(v_look, 1)
            link(nc.vector.tensor_single_scalar(inblk[:], iv("lens_col"), BLOCK - 1, ALU.bitwise_and))
            link(nc.vector.tensor_tensor(place[:], inblk[:], cv("offset"), ALU.add))
            nc.vector.tensor_single_scalar(slot_of[:], place[:], 4, ALU.arith_shift_right)
            link(nc.vector.tensor_single_scalar(off_of[:], place[:], BLOCK - 1, ALU.bitwise_and))
            link(nc.vector.tensor_tensor(hit[:], free(cv("look"), (1, LOOK), (0, NCOL)),
                                         free(slot_of[:], (0, LOOK), (1, NCOL)), ALU.is_equal))
            dve.wait_ge(p_look, 1)
            link(nc.vector.tensor_tensor(hit[:], hit[:], looked_ps, ALU.mult))
            link(nc.vector.tensor_reduce(block_of[:], hit[:].rearrange("p j n -> p n j"), AX_X, ALU.add))
            link(nc.vector.scalar_tensor_tensor(out=row_of[:], in0=block_of[:], scalar=float(BLOCK), in1=off_of[:],
                                                op0=ALU.mult, op1=ALU.add))
            nc.vector.tensor_copy(hist_idx[:], row_of[:, 0:B]).then_inc(v_idx, 1)

            own = looked_ps[:, BACK:BACK + RUNS, 0:B]
            link(nc.vector.tensor_scalar(run_lo[:], own, float(BLOCK), None, ALU.mult))
            nc.vector.tensor_scalar(run_hi[:], run_lo[:], float(BLOCK), None, ALU.add)
            link(nc.vector.scalar_tensor_tensor(out=run_shift[:].rearrange("p i b -> p (i b)"),
                                                in0=run_lo[:].rearrange("p i b -> p (i b)"), scalar=-1.0,
                                                in1=cv("order"), op0=ALU.mult, op1=ALU.add))
            nc.vector.tensor_tensor(run_shift[:], run_shift[:], free(inblk[:, 0:B], (0, RUNS), (1, B)), ALU.subtract)
            nc.vector.tensor_tensor(run_hi[:, 2, :], run_lo[:, 2, :], inblk[:, 0:B], ALU.add)
            link(nc.vector.tensor_tensor(run_lo[:, 0, :], run_lo[:, 0, :], inblk[:, 0:B], ALU.add))

            dve.wait_ge(s_wb, 16)
            for c in range(C):
                w = Wb_sb[:, c, P * c:P * c + P]
                nc.vector.tensor_tensor(w, w, cv("ident"), ALU.add).then_inc(v_wb, 1)
            link(nc.vector.tensor_scalar(mask0[:], iv("adapter_idx", slice(0, ER)), cv("adapter", slice(0, ER)),
                                         cv("scaling", slice(0, ER)), ALU.is_equal, ALU.mult))
            for h in range(2):
                dve.wait_ge(p_z, h + 1)
                nc.vector.tensor_tensor(zm[:, 512 * h:512 * h + 512].rearrange("p (b t) -> p b t", t=T),
                                        z_ps[h][0:ER, :].rearrange("p (b t) -> p b t", t=T),
                                        free(mask0[:, 16 * h:16 * h + 16], (1, 16), (0, T)), ALU.mult).then_inc(v_zm, 1)

            link(nc.vector.tensor_scalar(pos[:], iv("lens_col")[:, B:NCOL], cv("t"), None, ALU.add))
            link(nc.vector.tensor_tensor(ang[:], free(pos[:], (1, TILES), (0, 2), (0, HALF)),
                                         free(cv("inv"), (0, TILES), (0, 2), (1, HALF)), ALU.mult))
            nc.vector.tensor_scalar(turns[:, :, 0, :], ang[:, :, 0, :], 1.0 / (2.0 * np.pi), 0.25, ALU.mult, ALU.add)
            link(nc.vector.tensor_scalar(turns[:, :, 1, :], ang[:, :, 1, :], 1.0 / (2.0 * np.pi), None, ALU.mult))
            link(nc.vector.tensor_scalar(turns[:], turns[:], MAGIC, MAGIC, ALU.add, ALU.subtract))
            flat = "p n s d -> p (n s d)"
            for part in TWO_PI:
                link(nc.vector.scalar_tensor_tensor(out=ang[:].rearrange(flat), in0=turns[:].rearrange(flat), scalar=-part,
                                                    in1=ang[:].rearrange(flat), op0=ALU.mult, op1=ALU.add))
            link(nc.vector.tensor_scalar(ang[:, :, 0, :], ang[:, :, 0, :], float(np.pi / 2), None, ALU.add))
            nc.vector.tensor_scalar(ang[:], ang[:], PI_SAFE, -PI_SAFE, ALU.min, ALU.max).then_inc(v_ang, 1)

            def writers(cols):
                n = len(cols)
                for s, c in enumerate(cols):
                    last = nc.vector.scalar_tensor_tensor(
                        out=above[:, s, :], in0=run_lo[:].rearrange("p i b -> p (i b)"), scalar=row_of[:, c:c + 1],
                        in1=run_shift[:].rearrange("p i b -> p (i b)"), op0=ALU.is_le, op1=ALU.mult)
                link(last)
                for s, c in enumerate(cols):
                    last = nc.vector.scalar_tensor_tensor(
                        out=match[:, s, :], in0=run_hi[:].rearrange("p i b -> p (i b)"), scalar=row_of[:, c:c + 1],
                        in1=above[:, s, :], op0=ALU.is_gt, op1=ALU.mult)
                link(last)
                link(nc.vector.tensor_reduce(best[:, cols[0]:cols[0] + n], match[:, 0:n, :], AX_X, ALU.max))

            groups = [list(range(s, s + 5)) for s in range(0, NCOL, 5)]
            early = len(groups) - TILES // 2
            for cols in groups[:2]:
                writers(cols)

            dve.wait_ge(s_bd2, 16 * BT)
            nc.vector.tensor_tensor(bd2[:], bd2[:], free(cv("ident"), (0, TILES), (1, P)), ALU.add).then_inc(v_B2, 1)
            for cols in groups[2:early]:
                writers(cols)
            for h in range(2):
                dve.wait_ge(p_M, h + 1)
                nc.vector.tensor_tensor(M_sb[:, 4 * h:4 * h + 4, :], M_ps[h], bd2[:, 4 * h:4 * h + 4, :],
                                        ALU.add).then_inc(v_M, 1)

            nc.vector.tensor_scalar(plus1[:, 0, :], cv("q_scale"), 1.0, SCALE, ALU.add, ALU.mult)
            link(nc.vector.tensor_scalar(plus1[:, 1, :], cv("k_scale"), 1.0, None, ALU.add))
            nc.vector.tensor_copy(cross1[:, :, 0:HALF], plus1[:, :, 0:HALF])
            link(nc.vector.tensor_scalar(cross1[:, :, HALF:HD], plus1[:, :, HALF:HD], -1.0, None, ALU.mult))
            dve.wait_ge(a_sin, 1)
            for w in range(2):
                for table, scale, fn in ((rot_same, plus1, 0), (rot_cross, cross1, 1)):
                    last = nc.vector.tensor_tensor(free(table[:, 0, w, :], (2 * HD, TILES), (HALF, 2), (1, HALF)),
                                                   free(cossin[:, 0, fn, :], (2 * HALF, TILES), (0, 2), (1, HALF)),
                                                   free(scale[:, w, :], (0, TILES), (HALF, 2), (1, HALF)), ALU.mult)
            link(last)

            for j in range(TILES // 2):
                dve.wait_ge(a_ksq, 2 * j + 2)
                two, at = slice(2 * j, 2 * j + 2), 2 * j % 4
                nc.vector.tensor_reduce(ssum[:, two, HH * G:HEADS], sq[:, at:at + 2, 0:KW].rearrange("p i (g d) -> p i g d", d=HD),
                                        AX_X, ALU.add).then_inc(v_ksum, 1)
                writers(groups[early + j])
                dve.wait_ge(a_kroot, j + 1)
                link(nc.vector.reciprocal(rnorm[:, two, HH * G:HEADS], root[:, two, HH * G:HEADS]))
                k = qkv[:, two, QW:QW + KW].rearrange("p i (g d) -> p i g d", d=HD)
                link(nc.vector.tensor_tensor(kn[:], k, free(rnorm[:, 2 * j, HH * G:HEADS], (HEADS, 2), (1, G), (0, HD)), ALU.mult))
                nc.vector.tensor_tensor(ks_[:], kn[:], free(rot_same[:, 2 * j, 1, :], (2 * HD, 2), (0, G), (1, HD)), ALU.mult)
                link(nc.vector.tensor_tensor(kc[:], kn[:], free(rot_cross[:, 2 * j, 1, :], (2 * HD, 2), (0, G), (1, HD)), ALU.mult))
                link(nc.vector.tensor_tensor(k[:, :, :, 0:HALF], ks_[:, :, :, 0:HALF], kc[:, :, :, HALF:HD], ALU.add))
                nc.vector.tensor_tensor(k[:, :, :, HALF:HD], ks_[:, :, :, HALF:HD], kc[:, :, :, 0:HALF], ALU.add).then_inc(v_k, 1)

            link(nc.vector.tensor_single_scalar(nobody[:], best[:], 0.0, ALU.is_equal))
            link(nc.vector.scalar_tensor_tensor(out=nobody[:], in0=nobody[:], scalar=NONE, in1=row_of[:], op0=ALU.mult, op1=ALU.add))
            link(nc.vector.tensor_tensor(best[:], best[:], nobody[:], ALU.add))
            nc.vector.tensor_scalar(patch_idx[:], best[:], -BIAS, None, ALU.add).then_inc(v_patch, 1)

            dve.wait_ge(z_misc, 2)
            link(nc.vector.tensor_scalar(lens_dyn[32:64, :], iv("lens_rb", slice(32, 64)), -1.0, float(WINDOW), ALU.mult, ALU.add))
            nc.vector.tensor_scalar(maskr[32:64, 0:WINDOW], cv("key", slice(32, 64)), lens_dyn[32:64, 0:1], MASKED,
                                    ALU.is_lt, ALU.mult).then_inc(v_dyn, 1)

            for j in range(TILES // 2):
                dve.wait_ge(a_qsq, 2 * j + 2)
                two, at = slice(2 * j, 2 * j + 2), 2 * j % 4
                nc.vector.tensor_reduce(ssum[:, two, 0:HH * G], sq[:, at:at + 2, :].rearrange("p i (g d) -> p i g d", d=HD),
                                        AX_X, ALU.add).then_inc(v_qsum, 1)
            dve.wait_ge(a_qroot, 1)
            link(nc.vector.reciprocal(rnorm[:, :, 0:HH * G], root[:, :, 0:HH * G]))

            def queries(i, step):
                q = qkv[:, i, 0:QW].rearrange("p (h d) -> p h d", d=HD)
                if step == 0:
                    link(nc.vector.tensor_tensor(qn[:], q, free(rnorm[:, i, 0:HH * G], (1, HH * G), (0, HD)), ALU.mult))
                if step == 1:
                    link(nc.vector.tensor_tensor(qs_[:], qn[:], free(rot_same[:, i, 0, :], (0, HH * G), (1, HD)), ALU.mult))
                if step == 2:
                    link(nc.vector.tensor_tensor(qc[:], qn[:], free(rot_cross[:, i, 0, :], (0, HH * G), (1, HD)), ALU.mult))
                if step == 3:
                    link(nc.vector.tensor_tensor(q[:, :, 0:HALF], qs_[:, :, 0:HALF], qc[:, :, HALF:HD], ALU.add))
                    nc.vector.tensor_tensor(q[:, :, HALF:HD], qs_[:, :, HALF:HD], qc[:, :, 0:HALF], ALU.add).then_inc(v_q, 1)

            def kq_out(g):
                dve.wait_ge(p_kq, g + 1)
                if g >= 2:
                    dve.wait_ge(p_s, BT * (g - 1))
                nc.vector.tensor_copy(KT[:, g % 2, :, WINDOW:KEYS], KTn_ps.rearrange("p (b t) -> p b t", b=BT)).then_inc(v_kn, 1)
                if g == 0:
                    dve.wait_ge(z_misc, 4)
                for j in range(G):
                    rows = slice(HD * j, HD * j + HD)
                    last = nc.vector.tensor_copy(qbd[rows, g % 2, :, j, :],
                                                 bank[5][rows, P:P + HH * P].rearrange("p (n t) -> p n t", t=T))
                last.then_inc(v_qbd, 1)

            def max_of(n):
                dve.wait_ge(p_s, n + 1)
                if n >= 4:
                    dve.wait_ge(a_exp, HH * (n - 3))
                nc.vector.tensor_reduce(negmax[:, n % 4, :], S_ps[n % 2], AX_X, ALU.max, negate=True).then_inc(v_max, 1)

            def sums_of(g):
                dve.wait_ge(a_exp, HH * BT * (g + 1))
                if g >= 2:
                    dve.wait_ge(p_ptn, g - 1)
                link(nc.vector.reciprocal(rsum[:], esum[:, g % 2, :]))
                nc.vector.tensor_tensor(rdiag[:, g % 2, :, :], free(cv("t_eye"), (0, BT * HH), (1, T)),
                                        free(rsum[:], (1, BT * HH), (0, T)), ALU.mult).then_inc(v_rdiag, 1)

            def values_apart(g):
                dve.wait_ge(s_patch[g], PATCHED)
                if g >= 2:
                    dve.wait_ge(p_o, BT * (g - 1))
                for j in range(BT):
                    rows = slice(T * j, T * j + T)
                    last = nc.vector.tensor_copy(Vbd[rows, g % 2, j, :], qkv[rows, g, QW + KW:])
                last.then_inc(v_vbd, 1)

            def o_out(g):
                dve.wait_ge(p_o, BT * (g + 1))
                if g >= 2:
                    dve.wait_ge(p_res, g - 1)
                nc.vector.tensor_tensor(oT[:, g % 2, :, :, :].rearrange("p h b t -> p b h t"), O_ps,
                                        PTn[:, g % 2, HH * P:].rearrange("p (b h t) -> p b h t", b=BT, h=HH),
                                        ALU.mult).then_inc(v_o, 1)

            for i in range(2):
                for step in range(4):
                    queries(i, step)
            kq_out(0)
            for n in range(B + 7):
                g, k = divmod(n, BT)
                if n < B:
                    max_of(n)
                if g + 2 < TILES:
                    queries(g + 2, k)
                if k == 0 and 1 <= g <= TILES:
                    sums_of(g - 1)
                if k == 3 and g < TILES:
                    values_apart(g)
                if k == 2 and g + 1 < TILES:
                    kq_out(g + 1)
                if k == 1 and n >= 9:
                    o_out((n - 9) // BT)

        @block.tensor
        def _(pe):
            pe.wait_ge(s_low, 16)
            Wt_v, AT_v, Bo_v, Wp_v = lv("Wt"), lv("AT"), lv("Bo"), lv("WpT")
            for c in range(C):
                for j in range(C):
                    last = nc.tensor.matmul(AW_ps[:, c, :], Wt_v[:, j, P * c:P * c + P], AT_v[:, j, :],
                                            start=(j == 0), stop=(j == C - 1))
            last.then_inc(p_AW, 1)
            pe.wait_ge(v_look, 2)
            nc.tensor.matmul(looked_ps[:, :, 0:B], ones[:], look_all[:].rearrange("p m (r b) -> p (m r) b", b=B),
                             start=True, stop=True)
            nc.tensor.matmul(looked_ps[:, :, B:NCOL], cv("same"), look_own[:].rearrange("p m (r n) -> p (m r) n", n=TILES),
                             start=True, stop=True).then_inc(p_look, 1)
            for j in range(C):
                last = nc.tensor.matmul(C_ps, Bo_v[:, j, :], Wp_v[:, j, :], start=(j == 0), stop=(j == C - 1))
            last.then_inc(p_C, 1)
            pe.wait_ge(s_x, 16)
            pe.wait_ge(a_AW, 1)
            for h in range(2):
                for c in range(C):
                    last = nc.tensor.matmul(z_ps[h][0:ER, :], AW_sb[:, c, :], xT_sb[:, c, 512 * h:512 * h + 512],
                                            start=(c == 0), stop=(c == C - 1))
                last.then_inc(p_z, 1)
            pe.wait_ge(v_wb, C)
            pe.wait_ge(a_C, 1)
            for i in range(TILES):
                rows = slice(P * i, P * i + P)
                if i >= 3:
                    pe.wait_ge(a_x1, i - 2)
                for c in range(C):
                    nc.tensor.matmul(x1_ps[i % 3], xT_sb[:, c, rows], Wb_sb[:, c, :], start=(c == 0), stop=False)
                pe.wait_ge(v_zm, i // 4 + 1)
                nc.tensor.matmul(x1_ps[i % 3], zm[:, rows], C_sb[:], start=False, stop=True).then_inc(p_x1, 1)
            pe.wait_ge(s_bd1, 16 * BT)
            pe.wait_ge(v_B2, 1)
            for i in range(TILES):
                last = nc.tensor.matmul(M_ps[i // 4][:, i % 4, :], bd1[:, i, :], bd2[:, i, :], start=True, stop=True)
                if i % 4 == 3:
                    last.then_inc(p_M, 1)

            def mix(i):
                pe.wait_ge(v_M, i // 4 + 1)
                pe.wait_ge(a_x1, i + 1)
                if i >= 2:
                    pe.wait_ge(a_x3T, i - 1)
                elif i == 0:
                    pe.wait_ge(v_zm, 2)
                for c in range(C):
                    last = nc.tensor.matmul(x3T_ps[i % 2][:, c, :], x1[:, i, P * c:P * c + P], M_sb[:, i, :],
                                            start=True, stop=True)
                last.then_inc(p_x3T, 1)

            pe.wait_ge(s_qkvw, 16)
            mix(0)
            for i in range(TILES):
                if i + 1 < TILES:
                    mix(i + 1)
                pe.wait_ge(a_x3T, i + 1)
                if i >= 3:
                    pe.wait_ge(a_kv, i - 2)
                elif i == 0:
                    pe.wait_ge(a_x1, TILES)
                for c in range(C):
                    last = nc.tensor.matmul(kv_ps[i % 3], x3T[:, i, c, :], Wqkv_sb[:, c, QW:],
                                            start=(c == 0), stop=(c == C - 1))
                last.then_inc(p_kv, 1)
            for i in range(TILES):
                if i >= 3:
                    pe.wait_ge(a_qraw, i - 2)
                elif i == 0:
                    pe.wait_ge(v_M, 2)
                for c in range(C):
                    last = nc.tensor.matmul(q_ps[i % 3], x3T[:, i, c, :], Wqkv_sb[:, c, 0:QW],
                                            start=(c == 0), stop=(c == C - 1))
                last.then_inc(p_qraw, 1)

            def kq_in(g):
                pe.wait_ge(s_patch[g], PATCHED)
                if g >= 1:
                    pe.wait_ge(a_kt, g)
                else:
                    pe.wait_ge(a_qraw, TILES)
                for j in range(BT):
                    last = nc.tensor.transpose(KT_ps[:, j, :], hist[:, BT * g + j, 0:KW], cv("ident"))
                last.then_inc(p_kt, 1)
                if g >= 2:
                    pe.wait_ge(a_ptn, g - 1)
                elif g == 0:
                    pe.wait_ge(a_kv, TILES)
                pe.wait_ge(v_q, g + 1)
                nc.tensor.transpose(KTn_ps, qkv[:, g, QW:QW + KW], cv("ident"))
                for h in range(HH):
                    last = nc.tensor.transpose(qT_ps[:, h, :], qkv[:, g, KW * h:KW * h + KW], cv("ident"))
                last.then_inc(p_kq, 1)

            def scores(n):
                g, j = divmod(n, BT)
                if j == 0:
                    pe.wait_ge(a_kt, g + 1)
                    pe.wait_ge(v_kn, g + 1)
                    pe.wait_ge(v_qbd, g + 1)
                if n == 0:
                    pe.wait_ge(s_mask, 32)
                    pe.wait_ge(v_dyn, 1)
                if n >= 2:
                    pe.wait_ge(a_exp, HH * (n - 1))
                for h in range(HH):
                    nc.tensor.matmul(S_ps[n % 2][:, h, :], sel_sb[:, n, :], maskr[:], start=True, stop=False)
                    last = nc.tensor.matmul(S_ps[n % 2][:, h, :], qbd[:, g % 2, BT * h + j, :, :].rearrange("p g t -> p (g t)"),
                                            KT[:, g % 2, j, :], start=False, stop=True)
                last.then_inc(p_s, 1)

            def probs_in(n):
                pe.wait_ge(a_exp, HH * (n + 1))
                if n >= 2:
                    pe.wait_ge(a_pt, n - 1)
                elif n == 0:
                    pe.wait_ge(a_x3T, TILES)
                for h in range(HH):
                    last = nc.tensor.transpose(PT_ps[n % 2][:, h, :], Pr[:, n % 8, h, 0:WINDOW], cv("ident"))
                last.then_inc(p_pt, 1)

            def probs_new_in(g):
                if g + 1 < TILES:
                    pe.wait_ge(v_qbd, g + 2)
                for h in range(HH):
                    for j in range(BT):
                        nc.tensor.matmul(PTn_ps[T * j:T * j + T, h, :], Pr[:, (BT * g + j) % 8, h, WINDOW:KEYS], cv("ident"),
                                         start=True, stop=True)
                pe.wait_ge(v_rdiag, g + 1)
                nc.tensor.matmul(rsum_ps, cv("group"), rdiag[:, g % 2, :, :].rearrange("p n t -> p (n t)"),
                                 start=True, stop=True).then_inc(p_ptn, 1)

            def values(n):
                g, j = divmod(n, BT)
                pe.wait_ge(a_pt, n + 1)
                if j == 0:
                    pe.wait_ge(a_ptn, g + 1)
                    pe.wait_ge(v_vbd, g + 1)
                    if g >= 1:
                        pe.wait_ge(v_o, g)
                for part in range(2):
                    for k in range(G):
                        rows = slice(HD * k, HD * k + HD)
                        cols = slice(T * k, T * k + T)
                        if part == 0:
                            nc.tensor.matmul(O_ps[rows, j], hist[:, n, KW + HD * k:KW + HD * k + HD], PT[:, n % 8, :, cols],
                                             start=True, stop=False)
                        else:
                            last = nc.tensor.matmul(O_ps[rows, j], Vbd[:, g % 2, j, rows], PTn_v[:, g % 2, :, cols],
                                                    start=False, stop=True)
                last.then_inc(p_o, 1)

            def rows_out(g):
                if g >= 1:
                    pe.wait_ge(a_res, g)
                nc.tensor.matmul(res_ps, M_sb[:, g, :], x1[:, g, :], start=True, stop=False)
                pe.wait_ge(v_o, g + 1)
                for h in range(HH):
                    last = nc.tensor.matmul(res_ps, oT[:, g % 2, h, :, :].rearrange("p b t -> p (b t)"), Wo_sb[:, h, :],
                                            start=False, stop=(h == HH - 1))
                last.then_inc(p_res, 1)

            PTn_v = PTn[:, :, 0:HH * P].rearrange("p i (h k) -> p i h k", h=HH)
            kq_in(0)
            pe.wait_ge(s_wo, 16)
            for n in range(B + 7):
                g, k = divmod(n, BT)
                if n < B:
                    scores(n)
                if 2 <= n < B + 2:
                    probs_in(n - 2)
                if k == 2 and g + 1 < TILES:
                    kq_in(g + 1)
                if k == 1 and 1 <= g <= TILES:
                    probs_new_in(g - 1)
                if 6 <= n < B + 6:
                    values(n - 6)
                if k == 2 and n >= 10:
                    rows_out((n - 10) // BT)


def kernel(**inputs):
    import concourse.bacc as bacc
    from concourse.bass_utils import run_bass_kernel_spmd

    a = {k: np.asarray(v) for k, v in inputs.items()}
    lens = a["itok_B_37_3939"]

    def heads_last(w):
        return w.reshape(G, HH, HD, D).transpose(3, 1, 0, 2).reshape(D, QW)

    def by_position(blocks):
        return blocks.transpose(0, 2, 1, 3).reshape(-1, KW)

    def over_partitions(w):
        return w.reshape(C, P, -1).transpose(1, 0, 2).reshape(P, -1)

    def every(v):
        return np.tile(v[None], (P, 1))

    band, select = mask_constants()
    per_batch = [np.tile(v.reshape(B, -1), (P // B, 1)) for v in (
        lens, a["itok_B_0_7"], a["itok_B_1_198"], a["itok_Bx257_0_4111"])]
    arrays = {
        "ints": np.concatenate([every(lens), np.repeat(lens.reshape(TILES, BT).T, T, 0), *per_batch[:3],
                                every(a["itok_B_0_3"]), per_batch[3]], axis=1),
        "const": np.concatenate([constants()[:, :CONST["q_scale"][0]], every(a["L3_cond_q_norm_scale"]),
                                 every(a["L3_cond_k_norm_scale"]),
                                 np.tile(np.repeat(a["L0_cond_scaling"], R), P // ER)[:, None]], axis=1),
        "low": np.concatenate([over_partitions(w) for w in (
            a["L0_cond_Wt"], a["L0_cond_A"].reshape(ER, D).T,
            a["L0_cond_B_w"].transpose(1, 0, 2).reshape(D, ER), a["L0_cond_Wp"].T)], axis=1),
        "xT": over_partitions(a["x"].reshape(TOK, D).T),
        "WbT": over_partitions(a["L0_cond_W_base"].T),
        "W1T": a["L1_cond_weights"].transpose(0, 2, 1).reshape(-1, T * T),
        "W2": a["L2_cond_weights"].reshape(-1, T * T),
        "WqkvT": over_partitions(np.concatenate(
            [heads_last(a["L3_cond_Wq"]), a["L3_cond_Wk"].T, a["L3_cond_Wv"].T], axis=1)),
        "WoT": over_partitions(a["L3_cond_Wo"].reshape(D, G, HH, HD).transpose(2, 1, 3, 0).reshape(D, D)),
        "cache": np.concatenate([by_position(a["L3_cond_k_blocks"]), by_position(a["L3_cond_v_blocks"])], axis=1),
        "band": band,
        "select": select,
    }
    arrays = {k: np.ascontiguousarray(v) for k, v in arrays.items()}
    nc = bacc.Bacc("TRN2", target_bir_lowering=False, num_devices=1)
    args = [nc.dram_tensor(k, v.shape, mybir.dt.from_np(v.dtype), kind="ExternalInput").ap() for k, v in arrays.items()]
    for name, shape in (("new_rows", [TOK, 2 * KW]), ("w1_rows", [B, T * T]), ("w2_rows", [B, T * T])):
        args.append(nc.dram_tensor(name, shape, F32, kind="Internal").ap())
    args.append(nc.dram_tensor("out", [TOK, D], F32, kind="ExternalOutput").ap())
    cond_resid_kernel(nc, *args)
    got = run_bass_kernel_spmd(nc, [arrays], core_ids=[0])
    return got.results[0]["out"].reshape(B, T, D)
```

```python
from contextlib import ExitStack

import concourse.bass as bass
import numpy as np
from concourse import mybir

ALU = mybir.AluOpType
ACT = mybir.ActivationFunctionType
F32 = mybir.dt.float32
BF16 = mybir.dt.bfloat16
I32 = mybir.dt.int32
U32 = mybir.dt.uint32
U16 = mybir.dt.uint16
AX_X = mybir.AxisListType.X

B, T, D = 32, 32, 256
P = 128
BT = P // T
TILES = B // BT
TOK = B * T
C = D // P
E, R = 4, 16
ER = E * R
G, HH, HD = 4, 2, 32
HALF = HD // 2
KW = G * HD
QW = HH * KW
HEADS = G * HH + G
WINDOW = 128
BLOCK = 16
SLOTS = 257
LOOK = 12
BACK = WINDOW // BLOCK
RUNS = 3
NCOL = B + TILES
COLS_AT_ONCE = 5
POOL_COLS = 20
KEYS = WINDOW + T
STEP_W = HH * WINDOW + KEYS
EPS = 1e-6
SCALE = float(D) ** -0.5
MASKED = -1e30
BIAS = float(1 << 17)
NONE = float(1 << 20)
MAGIC = 12582912.0
TWO_PI = (6.28125, 0.0019350051879882812, 3.019916050561552e-07)
PI_SAFE = 3.1415925
AHEAD = 5

CONST = {}
_at = 0
for _name, _n in (("ident", P), ("slot", SLOTS), ("look", LOOK), ("target", 3), ("offset", NCOL),
                  ("t", 1), ("inv", HALF), ("same", P), ("pick", 4 * TILES), ("adapter", 1),
                  ("order", RUNS * B), ("key", WINDOW), ("group", P), ("t_eye", T),
                  ("q_scale", HD), ("k_scale", HD), ("scaling", 1)):
    CONST[_name] = (_at, _n)
    _at += _n
CONST_W = _at

INTS = {"lens_col": (0, NCOL), "lens_rb": (NCOL, 1), "w1_idx": (NCOL + 1, 1), "w2_idx": (NCOL + 2, 1),
        "adapter_idx": (NCOL + 3, B), "table": (NCOL + 3 + B, SLOTS)}
INTS_W = NCOL + 3 + B + SLOTS
LOW = {"Wt": (0, D), "AT": (C * D, ER), "Bo": (C * (D + ER), ER), "WpT": (C * (D + 2 * ER), D)}
LOW_W = C * (2 * D + 2 * ER)


def constants():
    p = np.arange(P)
    c = np.zeros((P, CONST_W), np.float32)

    def put(name, v):
        a, n = CONST[name]
        c[:, a:a + n] = v

    put("ident", np.eye(P))
    put("slot", np.arange(SLOTS)[None])
    put("look", np.arange(LOOK)[None])
    put("target", (p // B)[:, None] + 4 * np.arange(3)[None] - BACK)
    put("offset", np.concatenate([np.repeat(p[:, None], B, 1), np.repeat(WINDOW + p[:, None] % T, TILES, 1)], 1))
    put("t", (p % T)[:, None])
    put("inv", (np.float32(1.0) / np.float32(10000.0) ** (np.arange(HALF, dtype=np.float32) / np.float32(HALF)))[None])
    put("same", ((p[:, None] % B) % BT == p[None] // T))
    rb = np.arange(4 * TILES)
    put("pick", (p[:, None] // B == rb[None] // TILES) & ((p[:, None] % B) // BT == rb[None] % TILES))
    put("adapter", (p // R)[:, None])
    i, b = np.arange(RUNS * B) // B, np.arange(RUNS * B) % B
    put("order", (T * b + BLOCK * i)[None] + BIAS - 0.5)
    put("key", np.arange(WINDOW)[None])
    put("group", p[:, None] // HD == p[None] // HD)
    put("t_eye", p[:, None] % T == np.arange(T)[None])
    return c


def mask_constants():
    t, key = np.arange(T)[:, None], np.arange(KEYS)[None]
    band = np.where((key > t) & (key <= t + WINDOW), 0.0, MASKED)
    sel = np.zeros((2, 32, B, G, T))
    sel[0] = np.eye(T)[:, None, None, :]
    sel[1] = np.eye(B)[:, :, None, None]
    return [(v.astype(np.float32).view(np.uint32) >> 16).astype(np.uint16) for v in (band, sel.reshape(64, B * P))]


def free(ap, *dims):
    return bass.AP(tensor=ap.tensor, offset=ap.offset, ap=[list(ap.ap[0])] + [list(d) for d in dims])


def dram(ap, *dims):
    return bass.AP(tensor=ap.tensor, offset=ap.offset, ap=[list(d) for d in dims])


def cond_resid_kernel(nc, ints, const, low, xT, WbT, W1T, W2, WqkvT, WoT, cache, band, select,
                      new_rows, w1_rows, w2_rows, out):
    with ExitStack() as ctx:
        def sb(name, shape, dt=F32):
            return ctx.enter_context(nc.sbuf_tensor(name, shape, dt))

        def sem(name):
            return ctx.enter_context(nc.semaphore(name))

        bank = [ctx.enter_context(nc.psum_tensor(f"bank{i}", [P, 512], F32)) for i in range(8)]

        cst = sb("cst", [P, CONST_W])
        ints_sb = sb("ints_sb", [P, INTS_W], I32)
        low_sb = sb("low_sb", [P, LOW_W])
        lens_dyn = sb("lens_dyn", [64, 1])
        xT_sb = sb("xT_sb", [P, C, TOK])
        Wb_sb = sb("Wb_sb", [P, C, D])
        Wqkv_sb = sb("Wqkv_sb", [P, C, QW + 2 * KW])
        Wo_sb = sb("Wo_sb", [P, HH, D])
        maskr = sb("maskr", [P, KEYS], BF16)
        sel_sb = sb("sel_sb", [P, B, P], BF16)

        slot0 = sb("slot0", [P, 1], I32)
        target = sb("target", [P, 3])
        junk = sb("junk", [P, 3, SLOTS])
        looked = sb("looked", [P, 3])
        look_all = sb("look_all", [P, 3, P])
        look_own = sb("look_own", [P, 3, 4 * TILES])
        ones = sb("ones", [P, P])
        eps = sb("eps", [P, 1])
        inblk = sb("inblk", [P, NCOL], I32)
        place = sb("place", [P, NCOL], I32)
        slot_of = sb("slot_of", [P, NCOL], I32)
        off_of = sb("off_of", [P, NCOL], I32)
        hit = sb("hit", [P, LOOK, NCOL])
        block_of = sb("block_of", [P, NCOL])
        row_of = sb("row_of", [P, NCOL])
        hist_idx = sb("hist_idx", [P, B], I32)
        run_lo = sb("run_lo", [P, RUNS, B])
        run_hi = sb("run_hi", [P, RUNS, B])
        run_shift = sb("run_shift", [P, RUNS, B])
        best = sb("best", [P, NCOL])
        nobody = sb("nobody", [P, NCOL])
        patch_idx = sb("patch_idx", [P, NCOL], I32)

        pos = sb("pos", [P, TILES])
        ang = sb("ang", [P, TILES, 2, HALF])
        turns = sb("turns", [P, TILES, 2, HALF])
        cossin = sb("cossin", [P, TILES, 2, HALF])
        plus1 = sb("plus1", [P, 2, HD])
        cross1 = sb("cross1", [P, 2, HD])
        rot_same = sb("rot_same", [P, TILES, 2, HD])
        rot_cross = sb("rot_cross", [P, TILES, 2, HD])

        mask0 = sb("mask0", [ER, B])
        AW_sb = sb("AW_sb", [P, C, ER])
        C_sb = sb("C_sb", [ER, D])
        zm = sb("zm", [ER, TOK])
        w1_sb = sb("w1_sb", [B, T * T])
        w2_sb = sb("w2_sb", [B, T * T])
        bd1 = sb("bd1", [P, TILES, P])
        bd2 = sb("bd2", [P, TILES, P])
        M_sb = sb("M_sb", [P, TILES, P])
        x1 = sb("x1", [P, TILES, D])
        x3T = sb("x3T", [P, TILES, C, P])

        qkv = sb("qkv", [P, TILES, QW + 2 * KW])
        sq = sb("sq", [P, 4, QW])
        ssum = sb("ssum", [P, TILES, HEADS])
        root = sb("root", [P, TILES, HEADS])
        rnorm = sb("rnorm", [P, TILES, HEADS])
        normed = sb("normed", [P, 2 * QW])
        same = sb("same", [P, 2 * QW])
        cross = sb("cross", [P, 2 * QW])
        unread = sb("unread", [P, 1])
        hist = sb("hist", [P, B, 2 * KW])
        qbd = sb("qbd", [P, 2, HH * BT, G, T])
        Vbd = sb("Vbd", [P, 2, BT, KW])
        negmax = sb("negmax", [P, 4, HH])
        esum = sb("esum", [P, 2, BT * HH])
        rsum = sb("rsum", [P, BT * HH])
        rdiag = sb("rdiag", [P, 2, BT * HH, T])
        shared = sb("shared", [P, 8 * (HH * KEYS + STEP_W)])
        Pr = shared[:, 0:8 * HH * KEYS].rearrange("p (n h k) -> p n h k", n=8, h=HH)
        ring = shared[:, 8 * HH * KEYS:].rearrange("p (n k) -> p n k", n=8)
        above = shared[:, 0:NCOL * RUNS * B].rearrange("p (n j) -> p n j", n=NCOL)
        below = shared[:, NCOL * RUNS * B:(NCOL + POOL_COLS) * RUNS * B].rearrange("p (n j) -> p n j", n=POOL_COLS)
        PTn = sb("PTn", [P, 2, 2 * HH * P])
        oT = sb("oT", [P, 2, HH, BT, T])
        res = sb("res", [P, 2, D])

        def cv(name, rows=slice(0, P)):
            a, n = CONST[name]
            return cst[rows, a:a + n]

        def iv(name, rows=slice(0, P)):
            a, n = INTS[name]
            return ints_sb[rows, a:a + n]

        def lv(name):
            a, n = LOW[name]
            return low_sb[:, a:a + C * n].rearrange("p (c n) -> p c n", c=C)

        s_int, s_cst, s_low, s_x, s_wb, s_qkvw, s_wo, s_mask = map(sem, (
            "s_int", "s_cst", "s_low", "s_x", "s_wb", "s_qkvw", "s_wo", "s_mask"))
        s_w1g, s_w2g, s_w1d, s_w2d, s_bd1, s_bd2 = map(sem, ("s_w1g", "s_w2g", "s_w1d", "s_w2d", "s_bd1", "s_bd2"))
        s_new = sem("s_new")
        s_hist = [sem(f"s_hist{g}") for g in range(TILES)]
        s_patch = [sem(f"s_patch{g}") for g in range(TILES)]
        s_out = [sem(f"s_out{g}") for g in range(2)]
        z_bd, z_misc = sem("z_bd"), sem("z_misc")
        v_chain = sem("v_chain")
        g_chain, g_ang, g_rot, g_B2, g_run = map(sem, ("g_chain", "g_ang", "g_rot", "g_B2", "g_run"))
        v_look, v_ang, v_idx, v_run, v_patch, v_wb, v_zm, v_scale, v_M, v_dyn = map(sem, (
            "v_look", "v_ang", "v_idx", "v_run", "v_patch", "v_wb", "v_zm", "v_scale", "v_M", "v_dyn"))
        v_ksum, v_k, v_qsum, v_q, v_max, v_qbd, v_vbd, v_rdiag, v_o, v_res = map(sem, (
            "v_ksum", "v_k", "v_qsum", "v_q", "v_max", "v_qbd", "v_vbd", "v_rdiag", "v_o", "v_res"))
        a_AW, a_C, a_x1, a_x3T, a_x3, a_kv, a_ksq, a_kroot, a_qraw, a_qsq, a_qroot, a_sin = map(sem, (
            "a_AW", "a_C", "a_x1", "a_x3T", "a_x3", "a_kv", "a_ksq", "a_kroot", "a_qraw", "a_qsq", "a_qroot", "a_sin"))
        a_exp, a_step, a_ptn = map(sem, ("a_exp", "a_step", "a_ptn"))
        p_look, p_AW, p_C, p_z, p_x1, p_M, p_x3T, p_x3, p_kv, p_qraw = map(sem, (
            "p_look", "p_AW", "p_C", "p_z", "p_x1", "p_M", "p_x3T", "p_x3", "p_kv", "p_qraw"))
        p_qT, p_s, p_step, p_ptn, p_o, p_res = map(sem, ("p_qT", "p_s", "p_step", "p_ptn", "p_o", "p_res"))

        looked_ps = bank[0][:, 0:LOOK * NCOL].rearrange("p (j n) -> p j n", j=LOOK)
        AW_ps = bank[1][:, 0:C * ER].rearrange("p (c n) -> p c n", c=C)
        C_ps = bank[2][0:ER, 0:D]
        z_ps = [bank[3], bank[4]]
        x1_ps = [bank[5][:, 0:D], bank[6][:, 0:D], bank[7][:, 0:D]]
        M_ps = [bank[1][:, :].rearrange("p (i n) -> p i n", i=4), bank[2][:, :].rearrange("p (i n) -> p i n", i=4)]
        x3T_ps = [bank[3][:, 0:D].rearrange("p (c n) -> p c n", c=C), bank[4][:, 0:D].rearrange("p (c n) -> p c n", c=C)]
        x3_ps = [bank[3][:, 0:D], bank[4][:, 0:D]]
        kv_ps = [bank[i][:, 0:2 * KW] for i in (5, 6, 7)]
        q_ps = [bank[i][:, 0:QW] for i in (0, 1, 2)]

        S_ps = [bank[i][:, 0:HH * KEYS].rearrange("p (h k) -> p h k", h=HH) for i in (0, 1)]
        qT_ps = bank[2][:, 0:HH * P].rearrange("p (h k) -> p h k", h=HH)
        step_ps = [bank[3][:, 0:STEP_W], bank[4][:, 0:STEP_W]]
        PTn_ps = bank[5][:, 0:HH * P].rearrange("p (h k) -> p h k", h=HH)
        rsum_ps = bank[5][:, HH * P:2 * HH * P]
        O_ps = bank[6][:, 0:BT * HH * T].rearrange("p (b h t) -> p b h t", b=BT, h=HH)
        res_ps = bank[7][:, 0:D]

        block = ctx.enter_context(nc.Block())

        PATCHED = 16 * (BT + 1)

        @block.sync
        def _(sp):
            sp.dma_start(ints_sb[:], ints).then_inc(s_int, 16)
            sp.dma_start(low_sb[:], low).then_inc(s_low, 16)
            sp.dma_start(Wb_sb[:], WbT.rearrange("p (c n) -> p c n", c=C)).then_inc(s_wb, 16)
            for got, gathered, rows, wrote in ((s_w1g, w1_sb, w1_rows, s_w1d), (s_w2g, w2_sb, w2_rows, s_w2d)):
                sp.wait_ge(got, 16)
                sp.dma_start(rows, gathered[:]).then_inc(wrote, 16)
            sp.wait_ge(z_bd, 2)
            for rows, wrote, bd, done in ((w2_rows, s_w2d, bd2, s_bd2), (w1_rows, s_w1d, bd1, s_bd1)):
                sp.wait_ge(wrote, 16)
                for j in range(BT):
                    src = rows.rearrange("(n j) (k c) -> j k n c", j=BT, k=T)[j]
                    sp.dma_start(bd[T * j:T * j + T, :, T * j:T * j + T], src).then_inc(done, 16)
            sp.dma_start(Wo_sb[:], WoT.rearrange("p (h n) -> p h n", h=HH)).then_inc(s_wo, 16)
            new_tiles = new_rows.rearrange("(i p) n -> p i n", p=P)
            for j in range(TILES // 2):
                sp.wait_ge(v_k, j + 1)
                sp.wait_ge(a_kv, 2 * j + 2)
                sp.dma_start(new_tiles[:, 2 * j:2 * j + 2, :], qkv[:, 2 * j:2 * j + 2, QW:]).then_inc(s_new, 16)
            for i in range(TILES):
                sp.wait_ge(v_res, i + 1)
                sp.dma_start(out[P * i:P * i + P, :], res[:, i % 2, :]).then_inc(s_out[i % 2], 16)
            sp.wait_ge(s_out[0], 16 * (TILES // 2))
            sp.wait_ge(s_out[1], 16 * (TILES // 2))

        @block.gpsimd
        def _(pool):
            count = [0]

            def link(ins):
                count[0] += 1
                ins.then_inc(g_chain, 1)
                pool.wait_ge(g_chain, count[0])

            nc.gpsimd.memset(bd1[:], 0.0).then_inc(z_bd, 1)
            nc.gpsimd.memset(bd2[:], 0.0).then_inc(z_bd, 1)
            pool.wait_ge(s_int, 16)
            for rows, table, name, got in ((w1_sb, W1T, "w1_idx", s_w1g), (w2_sb, W2, "w2_idx", s_w2g)):
                nc.gpsimd.indirect_dma_start(
                    rows[:], None, table,
                    bass.IndirectOffsetOnAxis(ap=iv(name, slice(0, B)).bitcast(U32), axis=0)).then_inc(got, 16)

            pool.wait_ge(s_cst, 16)
            link(nc.gpsimd.tensor_scalar(pos[:], iv("lens_col")[:, B:NCOL], cv("t"), None, ALU.add))
            link(nc.gpsimd.tensor_tensor(ang[:], free(pos[:], (1, TILES), (0, 2), (0, HALF)),
                                         free(cv("inv"), (0, TILES), (0, 2), (1, HALF)), ALU.mult))
            nc.gpsimd.tensor_scalar(turns[:, :, 0, :], ang[:, :, 0, :], 1.0 / (2.0 * np.pi), 0.25, ALU.mult,
                                    ALU.add).then_inc(g_ang, 1)
            nc.gpsimd.tensor_scalar(turns[:, :, 1, :], ang[:, :, 1, :], 1.0 / (2.0 * np.pi), None,
                                    ALU.mult).then_inc(g_ang, 1)

            def gather(i):
                for b in range(BT * i, BT * i + BT):
                    nc.gpsimd.indirect_dma_start(
                        hist[:, b, :], None, cache,
                        bass.IndirectOffsetOnAxis(ap=hist_idx[:, b:b + 1].bitcast(U32), axis=0)).then_inc(s_hist[i], 16)

            def patch(i):
                nc.gpsimd.indirect_dma_start(
                    qkv[:, i, QW:], None, new_rows,
                    bass.IndirectOffsetOnAxis(ap=patch_idx[:, B + i:B + i + 1].bitcast(U32), axis=0),
                    bounds_check=TOK - 1, oob_is_err=False).then_inc(s_patch[i], 16)
                pool.wait_ge(s_hist[i], 16 * BT)
                for b in range(BT * i, BT * i + BT):
                    nc.gpsimd.indirect_dma_start(
                        hist[:, b, :], None, new_rows,
                        bass.IndirectOffsetOnAxis(ap=patch_idx[:, b:b + 1].bitcast(U32), axis=0),
                        bounds_check=TOK - 1, oob_is_err=False).then_inc(s_patch[i], 16)

            pool.wait_ge(g_ang, 2)
            nc.gpsimd.memset(sel_sb[64:P, :, :].bitcast(F32), 0.0).then_inc(z_misc, 1)
            pool.wait_ge(z_misc, 1)
            nc.gpsimd.memset(maskr[:].bitcast(F32), 0.0).then_inc(z_misc, 1)
            nc.gpsimd.memset(qbd[:], 0.0).then_inc(z_misc, 1)
            nc.gpsimd.memset(Vbd[:], 0.0).then_inc(z_misc, 1)
            pool.wait_ge(v_idx, 1)
            gather(0)
            pool.wait_ge(v_scale, 1)
            pool.wait_ge(a_sin, 1)
            for w in range(2):
                for table, scale, fn in ((rot_same, plus1, 0), (rot_cross, cross1, 1)):
                    nc.gpsimd.tensor_tensor(free(table[:, 0, w, :], (2 * HD, TILES), (HALF, 2), (1, HALF)),
                                            free(cossin[:, 0, fn, :], (2 * HALF, TILES), (0, 2), (1, HALF)),
                                            free(scale[:, w, :], (0, TILES), (HALF, 2), (1, HALF)), ALU.mult).then_inc(g_rot, 1)
            pool.wait_ge(s_bd2, 16 * BT)
            nc.gpsimd.tensor_tensor(bd2[:], bd2[:], free(cv("ident"), (0, TILES), (1, P)), ALU.add).then_inc(g_B2, 1)
            for i in range(1, AHEAD - 2):
                gather(i)
            pool.wait_ge(v_run, 1)
            last_cols = slice(NCOL - POOL_COLS, NCOL)
            mine = above[:, last_cols, :]
            row = free(row_of[:, last_cols], (1, POOL_COLS), (0, RUNS * B))

            def per_run(v):
                return free(v[:], (0, POOL_COLS), (1, RUNS * B))

            nc.gpsimd.tensor_tensor(mine, row, per_run(run_lo), ALU.subtract)
            link(nc.gpsimd.tensor_tensor(below, per_run(run_hi), row, ALU.subtract))
            nc.gpsimd.tensor_tensor(mine, mine, below, ALU.mult).then_inc(g_run, 1)
            gather(AHEAD - 2)
            gather(AHEAD - 1)
            pool.wait_ge(v_patch, 1)
            pool.wait_ge(s_new, 16 * (TILES // 2))
            for i in range(TILES):
                patch(i)
                if i >= 1 and AHEAD + i - 1 < TILES:
                    gather(AHEAD + i - 1)

        @block.scalar
        def _(act):
            act.dma_start(cst[:], const).then_inc(s_cst, 16)
            act.dma_start(xT_sb[:], xT.rearrange("p (c n) -> p c n", c=C)).then_inc(s_x, 16)
            act.dma_start(Wqkv_sb[:], WqkvT.rearrange("p (c n) -> p c n", c=C)).then_inc(s_qkvw, 16)

            act.wait_ge(p_AW, 1)
            nc.scalar.copy(AW_sb[:], AW_ps).then_inc(a_AW, 1)
            act.wait_ge(p_C, 1)
            nc.scalar.copy(C_sb[:], C_ps).then_inc(a_C, 1)
            act.wait_ge(v_ang, 1)
            nc.scalar.activation(cossin[:], ang[:], ACT.Sin).then_inc(a_sin, 1)
            act.wait_ge(v_run, 1)
            nc.scalar.activation(unread[:], eps[:], ACT.Sqrt)
            for i in range(TILES):
                act.wait_ge(p_x1, i + 1)
                nc.scalar.copy(x1[:, i, :], x1_ps[i % 3]).then_inc(a_x1, 1)

            def k_root(j):
                act.wait_ge(v_ksum, j + 1)
                nc.scalar.activation(root[:, 2 * j:2 * j + 2, HH * G:HEADS], ssum[:, 2 * j:2 * j + 2, HH * G:HEADS],
                                     ACT.Sqrt, scale=1.0 / HD, bias=eps[:, 0:1]).then_inc(a_kroot, 1)

            for i in range(TILES + 1):
                if i < TILES:
                    act.wait_ge(p_x3T, i + 1)
                    nc.scalar.copy(x3T[:, i, :, :], x3T_ps[i % 2]).then_inc(a_x3T, 1)
                if i >= 1:
                    j = i - 1
                    act.wait_ge(p_kv, i)
                    nc.scalar.copy(qkv[:, j, QW:], kv_ps[j % 3]).then_inc(a_kv, 1)
                    if j >= 4 and j % 2 == 0:
                        act.wait_ge(v_ksum, j // 2 - 1)
                    act.wait_ge(a_kv, i)
                    nc.scalar.activation(sq[:, j % 4, 0:KW], qkv[:, j, QW:QW + KW], ACT.Square).then_inc(a_ksq, 1)
                    if j >= 2 and j % 2 == 0:
                        k_root(j // 2 - 1)
            k_root(TILES // 2 - 1)
            act.wait_ge(z_misc, 4)
            act.dma_start(sel_sb[0:64, :, :].bitcast(U16), select.rearrange("p (b n) -> p b n", b=B)).then_inc(s_mask, 16)
            act.dma_start(maskr[0:T, :].bitcast(U16), band).then_inc(s_mask, 16)
            def q_root(j):
                act.wait_ge(v_qsum, j + 1)
                nc.scalar.activation(root[:, 2 * j:2 * j + 2, 0:HH * G], ssum[:, 2 * j:2 * j + 2, 0:HH * G],
                                     ACT.Sqrt, scale=1.0 / HD, bias=eps[:, 0:1]).then_inc(a_qroot, 1)

            for j in range(TILES):
                act.wait_ge(p_qraw, j + 1)
                nc.scalar.copy(qkv[:, j, 0:QW], q_ps[j % 3]).then_inc(a_qraw, 1)
                if j >= 4 and j % 2 == 0:
                    act.wait_ge(v_qsum, j // 2 - 1)
                elif j == 0:
                    act.wait_ge(v_ksum, TILES // 2)
                act.wait_ge(a_qraw, j + 1)
                nc.scalar.activation(sq[:, j % 4, :], qkv[:, j, 0:QW], ACT.Square).then_inc(a_qsq, 1)
                act.wait_ge(p_x3, j + 1)
                nc.scalar.copy(x1[:, j, :], x3_ps[j % 2]).then_inc(a_x3, 1)
                if j >= 2 and j % 2 == 0:
                    q_root(j // 2 - 1)
            q_root(TILES // 2 - 1)
            nc.scalar.activation(unread[:], eps[:], ACT.Exp)

            def step_out(m):
                act.wait_ge(p_step, m + 3)
                if m >= 6:
                    act.wait_ge(p_s, m - 5)
                if m >= 10:
                    act.wait_ge(p_o, m - 9)
                cols = slice(0 if m >= 2 else HH * WINDOW, STEP_W if m + 2 < B else HH * WINDOW)
                nc.scalar.copy(ring[:, m % 8, cols], step_ps[m % 2][:, cols]).then_inc(a_step, 1)

            def exps(n):
                g, j = divmod(n, BT)
                act.wait_ge(v_max, n + 1)
                if n >= 8:
                    act.wait_ge(p_step, n - 3)
                    act.wait_ge(p_ptn, g - 1)
                    act.wait_ge(v_rdiag, g - 1)
                for h in range(HH):
                    nc.scalar.activation(Pr[:, n % 8, h, :], S_ps[n % 2][:, h, :], ACT.Exp, bias=negmax[:, n % 4, h:h + 1],
                                         accum_out=esum[:, g % 2, HH * j + h:HH * j + h + 1]).then_inc(a_exp, 1)

            def ptn_out(g):
                act.wait_ge(p_ptn, g + 1)
                if g >= 2:
                    act.wait_ge(p_o, BT * (g - 1))
                    act.wait_ge(v_o, g - 1)
                nc.scalar.copy(PTn[:, g % 2, :], bank[5][:, :]).then_inc(a_ptn, 1)

            step_out(-2)
            step_out(-1)
            for n in range(B + 7):
                g, k = divmod(n, BT)
                if n < B:
                    exps(n)
                if n < B + 2:
                    step_out(n)
                if k == 1 and 1 <= g <= TILES:
                    ptn_out(g - 1)

        @block.vector
        def _(dve):
            count = [0]

            def link(ins):
                count[0] += 1
                ins.then_inc(v_chain, 1)
                dve.wait_ge(v_chain, count[0])

            nc.vector.memset(eps[:], EPS)
            link(nc.vector.memset(ones[:], 1.0))
            dve.wait_ge(s_int, 16)
            link(nc.vector.tensor_single_scalar(slot0[:], iv("lens_rb"), 4, ALU.arith_shift_right))
            dve.wait_ge(s_cst, 16)
            link(nc.vector.tensor_scalar(target[:], cv("target"), slot0[:, 0:1], None, ALU.add))
            for m in range(3):
                last = nc.vector.scalar_tensor_tensor(out=junk[:, m, :], in0=cv("slot"), scalar=target[:, m:m + 1],
                                                      in1=iv("table"), op0=ALU.is_equal, op1=ALU.mult,
                                                      accum_out=looked[:, m:m + 1])
            link(last)
            nc.vector.tensor_tensor(look_all[:], free(cv("ident"), (0, 3), (1, P)), free(looked[:], (1, 3), (0, P)),
                                    ALU.mult).then_inc(v_look, 1)
            nc.vector.tensor_tensor(look_own[:], free(cv("pick"), (0, 3), (1, 4 * TILES)),
                                    free(looked[:], (1, 3), (0, 4 * TILES)), ALU.mult).then_inc(v_look, 1)
            link(nc.vector.tensor_single_scalar(inblk[:], iv("lens_col"), BLOCK - 1, ALU.bitwise_and))
            link(nc.vector.tensor_tensor(place[:], inblk[:], cv("offset"), ALU.add))
            nc.vector.tensor_single_scalar(slot_of[:], place[:], 4, ALU.arith_shift_right)
            link(nc.vector.tensor_single_scalar(off_of[:], place[:], BLOCK - 1, ALU.bitwise_and))
            link(nc.vector.tensor_tensor(hit[:], free(cv("look"), (1, LOOK), (0, NCOL)),
                                         free(slot_of[:], (0, LOOK), (1, NCOL)), ALU.is_equal))
            dve.wait_ge(g_ang, 2)
            link(nc.vector.tensor_scalar(turns[:], turns[:], MAGIC, MAGIC, ALU.add, ALU.subtract))
            flat = "p n s d -> p (n s d)"
            for part in TWO_PI:
                link(nc.vector.scalar_tensor_tensor(out=ang[:].rearrange(flat), in0=turns[:].rearrange(flat), scalar=-part,
                                                    in1=ang[:].rearrange(flat), op0=ALU.mult, op1=ALU.add))
            link(nc.vector.tensor_scalar(ang[:, :, 0, :], ang[:, :, 0, :], float(np.pi / 2), None, ALU.add))
            nc.vector.tensor_scalar(ang[:], ang[:], PI_SAFE, -PI_SAFE, ALU.min, ALU.max).then_inc(v_ang, 1)
            nc.vector.tensor_scalar(plus1[:, 0, :], cv("q_scale"), 1.0, SCALE, ALU.add, ALU.mult)
            link(nc.vector.tensor_scalar(plus1[:, 1, :], cv("k_scale"), 1.0, None, ALU.add))
            nc.vector.tensor_copy(cross1[:, :, 0:HALF], plus1[:, :, 0:HALF])
            nc.vector.tensor_scalar(cross1[:, :, HALF:HD], plus1[:, :, HALF:HD], -1.0, None, ALU.mult).then_inc(v_scale, 1)
            dve.wait_ge(p_look, 1)
            link(nc.vector.tensor_tensor(hit[:], hit[:], looked_ps, ALU.mult))
            link(nc.vector.tensor_reduce(block_of[:], hit[:].rearrange("p j n -> p n j"), AX_X, ALU.add))
            link(nc.vector.scalar_tensor_tensor(out=row_of[:], in0=block_of[:], scalar=float(BLOCK), in1=off_of[:],
                                                op0=ALU.mult, op1=ALU.add))
            nc.vector.tensor_copy(hist_idx[:], row_of[:, 0:B]).then_inc(v_idx, 1)

            own = looked_ps[:, BACK:BACK + RUNS, 0:B]
            link(nc.vector.tensor_scalar(run_lo[:], own, float(BLOCK), -0.5, ALU.mult, ALU.add))
            nc.vector.tensor_scalar(run_hi[:], run_lo[:], float(BLOCK), None, ALU.add)
            link(nc.vector.scalar_tensor_tensor(out=run_shift[:].rearrange("p i b -> p (i b)"),
                                                in0=run_lo[:].rearrange("p i b -> p (i b)"), scalar=-1.0,
                                                in1=cv("order"), op0=ALU.mult, op1=ALU.add))
            nc.vector.tensor_tensor(run_shift[:], run_shift[:], free(inblk[:, 0:B], (0, RUNS), (1, B)), ALU.subtract)
            nc.vector.tensor_tensor(run_hi[:, 2, :], run_lo[:, 2, :], inblk[:, 0:B], ALU.add)
            nc.vector.tensor_tensor(run_lo[:, 0, :], run_lo[:, 0, :], inblk[:, 0:B], ALU.add).then_inc(v_run, 1)
            dve.wait_ge(v_run, 1)

            dve.wait_ge(s_wb, 16)
            for c in range(C):
                w = Wb_sb[:, c, P * c:P * c + P]
                nc.vector.tensor_tensor(w, w, cv("ident"), ALU.add).then_inc(v_wb, 1)
            link(nc.vector.tensor_scalar(mask0[:], iv("adapter_idx", slice(0, ER)), cv("adapter", slice(0, ER)),
                                         cv("scaling", slice(0, ER)), ALU.is_equal, ALU.mult))
            for h in range(2):
                dve.wait_ge(p_z, h + 1)
                nc.vector.tensor_tensor(zm[:, 512 * h:512 * h + 512].rearrange("p (b t) -> p b t", t=T),
                                        z_ps[h][0:ER, :].rearrange("p (b t) -> p b t", t=T),
                                        free(mask0[:, 16 * h:16 * h + 16], (1, 16), (0, T)), ALU.mult).then_inc(v_zm, 1)

            def find(k):
                cols = range(COLS_AT_ONCE * k, COLS_AT_ONCE * k + COLS_AT_ONCE)
                for c in cols:
                    last = nc.vector.scalar_tensor_tensor(
                        out=above[:, c, :], in0=run_lo[:].rearrange("p i b -> p (i b)"), scalar=row_of[:, c:c + 1],
                        in1=run_shift[:].rearrange("p i b -> p (i b)"), op0=ALU.is_le, op1=ALU.mult)
                link(last)
                for c in cols:
                    last = nc.vector.scalar_tensor_tensor(
                        out=above[:, c, :], in0=run_hi[:].rearrange("p i b -> p (i b)"), scalar=row_of[:, c:c + 1],
                        in1=above[:, c, :], op0=ALU.is_gt, op1=ALU.mult)
                link(last)
                best_of(slice(cols[0], cols[0] + COLS_AT_ONCE))

            def best_of(cols):
                link(nc.vector.tensor_reduce(best[:, cols], above[:, cols, :], AX_X, ALU.max))

            find(0)
            find(1)
            for h in range(2):
                dve.wait_ge(p_M, h + 1)
                nc.vector.tensor_tensor(M_sb[:, 4 * h:4 * h + 4, :], M_ps[h], bd2[:, 4 * h:4 * h + 4, :],
                                        ALU.add).then_inc(v_M, 1)
                if h == 0:
                    find(2)

            find(3)

            def rotate(w, heads, j, steps=range(4)):
                two, first, start = slice(2 * j, 2 * j + 2), HH * G * w, QW * w
                x = qkv[:, two, start:start + heads * HD].rearrange("p i (g d) -> p i g d", d=HD)
                n, s_, c_ = (v[:, 0:2 * heads * HD].rearrange("p (i g d) -> p i g d", i=2, d=HD)
                             for v in (normed, same, cross))
                for step in steps:
                    if step == 0:
                        link(nc.vector.reciprocal(rnorm[:, two, first:first + heads], root[:, two, first:first + heads]))
                        last = nc.vector.tensor_tensor(
                            n, x, free(rnorm[:, 2 * j, first:first + heads], (HEADS, 2), (1, heads), (0, HD)), ALU.mult)
                    elif step == 1:
                        last = nc.vector.tensor_tensor(
                            s_, n, free(rot_same[:, 2 * j, w, :], (2 * HD, 2), (0, heads), (1, HD)), ALU.mult)
                    elif step == 2:
                        last = nc.vector.tensor_tensor(
                            c_, n, free(rot_cross[:, 2 * j, w, :], (2 * HD, 2), (0, heads), (1, HD)), ALU.mult)
                    else:
                        nc.vector.tensor_tensor(x[:, :, :, 0:HALF], s_[:, :, :, 0:HALF], c_[:, :, :, HALF:HD], ALU.add)
                        last = nc.vector.tensor_tensor(x[:, :, :, HALF:HD], s_[:, :, :, HALF:HD], c_[:, :, :, 0:HALF], ALU.add)
                    if step in (0, 2):
                        link(last)
                return last

            def square_sums(j, heads, first):
                two, at = slice(2 * j, 2 * j + 2), 2 * j % 4
                return nc.vector.tensor_reduce(ssum[:, two, first:first + heads],
                                               sq[:, at:at + 2, 0:heads * HD].rearrange("p i (g d) -> p i g d", d=HD),
                                               AX_X, ALU.add)

            def k_sums(j):
                dve.wait_ge(a_ksq, 2 * j + 2)
                square_sums(j, G, HH * G).then_inc(v_ksum, 1)

            dve.wait_ge(g_rot, 4)
            for j in range(TILES // 2):
                k_sums(j)
                dve.wait_ge(a_kroot, j + 1)
                rotate(1, G, j).then_inc(v_k, 1)

            dve.wait_ge(g_run, 1)
            share = above[:, NCOL - POOL_COLS:NCOL, :]
            link(nc.vector.scalar_tensor_tensor(out=share, in0=share, scalar=0.0,
                                                in1=free(run_shift[:], (0, POOL_COLS), (1, RUNS * B)),
                                                op0=ALU.is_gt, op1=ALU.mult))
            best_of(slice(NCOL - POOL_COLS, NCOL))
            link(nc.vector.tensor_single_scalar(nobody[:], best[:], 0.0, ALU.is_equal))
            link(nc.vector.scalar_tensor_tensor(out=nobody[:], in0=nobody[:], scalar=NONE, in1=row_of[:], op0=ALU.mult, op1=ALU.add))
            link(nc.vector.tensor_tensor(best[:], best[:], nobody[:], ALU.add))
            nc.vector.tensor_scalar(patch_idx[:], best[:], -BIAS, None, ALU.add).then_inc(v_patch, 1)

            dve.wait_ge(z_misc, 2)
            link(nc.vector.tensor_scalar(lens_dyn[32:64, :], iv("lens_rb", slice(32, 64)), -1.0, float(WINDOW), ALU.mult, ALU.add))
            nc.vector.tensor_scalar(maskr[32:64, 0:WINDOW], cv("key", slice(32, 64)), lens_dyn[32:64, 0:1], MASKED,
                                    ALU.is_lt, ALU.mult).then_inc(v_dyn, 1)

            def q_sums(j):
                dve.wait_ge(a_qsq, 2 * j + 2)
                square_sums(j, HH * G, 0).then_inc(v_qsum, 1)

            q_sums(0)
            q_sums(1)
            dve.wait_ge(a_qroot, 1)
            rotate(0, HH * G, 0).then_inc(v_q, 1)
            q_sums(2)
            q_sums(3)

            def qbd_out(g):
                dve.wait_ge(p_qT, g + 1)
                if g >= 2:
                    dve.wait_ge(p_s, BT * (g - 1))
                if g == 0:
                    dve.wait_ge(z_misc, 4)
                for j in range(G):
                    rows = slice(HD * j, HD * j + HD)
                    last = nc.vector.tensor_copy(qbd[rows, g % 2, :, j, :],
                                                 bank[2][rows, 0:HH * P].rearrange("p (n t) -> p n t", t=T))
                last.then_inc(v_qbd, 1)

            def max_of(n):
                dve.wait_ge(p_s, n + 1)
                if n >= 4:
                    dve.wait_ge(a_exp, HH * (n - 3))
                nc.vector.tensor_reduce(negmax[:, n % 4, :], S_ps[n % 2], AX_X, ALU.max, negate=True).then_inc(v_max, 1)

            def sums_of(g):
                dve.wait_ge(a_exp, HH * BT * (g + 1))
                if g >= 2:
                    dve.wait_ge(p_ptn, g - 1)
                link(nc.vector.reciprocal(rsum[:], esum[:, g % 2, :]))
                nc.vector.tensor_tensor(rdiag[:, g % 2, :, :], free(cv("t_eye"), (0, BT * HH), (1, T)),
                                        free(rsum[:], (1, BT * HH), (0, T)), ALU.mult).then_inc(v_rdiag, 1)

            def values_apart(g):
                dve.wait_ge(s_patch[g], PATCHED)
                if g >= 2:
                    dve.wait_ge(p_o, BT * (g - 1))
                for j in range(BT):
                    rows = slice(T * j, T * j + T)
                    last = nc.vector.tensor_copy(Vbd[rows, g % 2, j, :], qkv[rows, g, QW + KW:])
                last.then_inc(v_vbd, 1)

            def o_out(g):
                dve.wait_ge(p_o, BT * (g + 1))
                if g >= 2:
                    dve.wait_ge(p_res, g - 1)
                nc.vector.tensor_tensor(oT[:, g % 2, :, :, :].rearrange("p h b t -> p b h t"), O_ps,
                                        PTn[:, g % 2, HH * P:].rearrange("p (b h t) -> p b h t", b=BT, h=HH),
                                        ALU.mult).then_inc(v_o, 1)

            def res_out(g):
                dve.wait_ge(p_res, g + 1)
                if g >= 2:
                    dve.wait_ge(s_out[g % 2], 16 * (g // 2))
                elif g == 0:
                    dve.wait_ge(a_x3, TILES)
                nc.vector.tensor_tensor(res[:, g % 2, :], res_ps, x1[:, g, :], ALU.add).then_inc(v_res, 1)

            qbd_out(0)
            for n in range(B + 7):
                g, k = divmod(n, BT)
                if n < B:
                    max_of(n)
                j, step = n // 8 + 1, n % 8 // 2
                if n % 2 == 0 and j < TILES // 2 and n % 8 < 6:
                    if step == 0:
                        dve.wait_ge(a_qroot, j + 1)
                    last = rotate(0, HH * G, j, ((0,), (1, 2), (3,))[step])
                    if step == 2:
                        last.then_inc(v_q, 1)
                if k == 0 and 1 <= g <= TILES:
                    sums_of(g - 1)
                if k == 3 and g < TILES:
                    values_apart(g)
                if k == 2 and g + 1 < TILES:
                    qbd_out(g + 1)
                if k == 1 and n >= 9:
                    o_out((n - 9) // BT)
                if k == 2 and n >= 10:
                    res_out((n - 10) // BT)

        @block.tensor
        def _(pe):
            pe.wait_ge(s_low, 16)
            Wt_v, AT_v, Bo_v, Wp_v = lv("Wt"), lv("AT"), lv("Bo"), lv("WpT")
            for c in range(C):
                for j in range(C):
                    last = nc.tensor.matmul(AW_ps[:, c, :], Wt_v[:, j, P * c:P * c + P], AT_v[:, j, :],
                                            start=(j == 0), stop=(j == C - 1))
            last.then_inc(p_AW, 1)
            pe.wait_ge(v_look, 2)
            nc.tensor.matmul(looked_ps[:, :, 0:B], ones[:], look_all[:].rearrange("p m (r b) -> p (m r) b", b=B),
                             start=True, stop=True)
            nc.tensor.matmul(looked_ps[:, :, B:NCOL], cv("same"), look_own[:].rearrange("p m (r n) -> p (m r) n", n=TILES),
                             start=True, stop=True).then_inc(p_look, 1)
            for j in range(C):
                last = nc.tensor.matmul(C_ps, Bo_v[:, j, :], Wp_v[:, j, :], start=(j == 0), stop=(j == C - 1))
            last.then_inc(p_C, 1)
            pe.wait_ge(s_x, 16)
            pe.wait_ge(a_AW, 1)
            for h in range(2):
                for c in range(C):
                    last = nc.tensor.matmul(z_ps[h][0:ER, :], AW_sb[:, c, :], xT_sb[:, c, 512 * h:512 * h + 512],
                                            start=(c == 0), stop=(c == C - 1))
                last.then_inc(p_z, 1)
            pe.wait_ge(v_wb, C)
            pe.wait_ge(a_C, 1)
            for i in range(TILES):
                rows = slice(P * i, P * i + P)
                if i >= 3:
                    pe.wait_ge(a_x1, i - 2)
                for c in range(C):
                    nc.tensor.matmul(x1_ps[i % 3], xT_sb[:, c, rows], Wb_sb[:, c, :], start=(c == 0), stop=False)
                pe.wait_ge(v_zm, i // 4 + 1)
                nc.tensor.matmul(x1_ps[i % 3], zm[:, rows], C_sb[:], start=False, stop=True).then_inc(p_x1, 1)
                if i in (4, 5):
                    if i == 4:
                        pe.wait_ge(s_bd1, 16 * BT)
                        pe.wait_ge(g_B2, 1)
                    h = i - 4
                    for j in range(4 * h, 4 * h + 4):
                        last = nc.tensor.matmul(M_ps[h][:, j % 4, :], bd1[:, j, :], bd2[:, j, :], start=True, stop=True)
                    last.then_inc(p_M, 1)
            def mix(i):
                pe.wait_ge(v_M, i // 4 + 1)
                pe.wait_ge(a_x1, i + 1)
                if i >= 2:
                    pe.wait_ge(a_x3T, i - 1)
                elif i == 0:
                    pe.wait_ge(v_zm, 2)
                for c in range(C):
                    last = nc.tensor.matmul(x3T_ps[i % 2][:, c, :], x1[:, i, P * c:P * c + P], M_sb[:, i, :],
                                            start=True, stop=True)
                last.then_inc(p_x3T, 1)

            pe.wait_ge(s_qkvw, 16)
            mix(0)
            for i in range(TILES):
                if i + 1 < TILES:
                    mix(i + 1)
                pe.wait_ge(a_x3T, i + 1)
                if i >= 3:
                    pe.wait_ge(a_kv, i - 2)
                elif i == 0:
                    pe.wait_ge(a_x1, TILES)
                for c in range(C):
                    last = nc.tensor.matmul(kv_ps[i % 3], x3T[:, i, c, :], Wqkv_sb[:, c, QW:],
                                            start=(c == 0), stop=(c == C - 1))
                last.then_inc(p_kv, 1)
            for i in range(TILES):
                if i >= 3:
                    pe.wait_ge(a_qraw, i - 2)
                elif i == 0:
                    pe.wait_ge(v_M, 2)
                for c in range(C):
                    last = nc.tensor.matmul(q_ps[i % 3], x3T[:, i, c, :], Wqkv_sb[:, c, 0:QW],
                                            start=(c == 0), stop=(c == C - 1))
                last.then_inc(p_qraw, 1)
                if i >= 2:
                    pe.wait_ge(a_x3, i - 1)
                elif i == 0:
                    pe.wait_ge(a_x3T, TILES)
                nc.tensor.matmul(x3_ps[i % 2], M_sb[:, i, :], x1[:, i, :], start=True, stop=True).then_inc(p_x3, 1)

            def queries_in(g):
                pe.wait_ge(v_q, g // 2 + 1)
                if g >= 1:
                    pe.wait_ge(v_qbd, g)
                else:
                    pe.wait_ge(a_qraw, TILES)
                for h in range(HH):
                    last = nc.tensor.transpose(qT_ps[:, h, :], qkv[:, g, KW * h:KW * h + KW], cv("ident"))
                last.then_inc(p_qT, 1)

            def step_in(m):
                if m >= 0:
                    pe.wait_ge(a_step, m + 1)
                elif m == -2:
                    pe.wait_ge(a_x3, TILES)
                ps = step_ps[m % 2]
                if m + 2 < B:
                    g, j = divmod(m + 2, BT)
                    if j == 0:
                        pe.wait_ge(s_patch[g], PATCHED)
                    at = HH * WINDOW
                    nc.tensor.transpose(ps[:, at:at + WINDOW], hist[:, m + 2, 0:KW], cv("ident"))
                    last = nc.tensor.matmul(ps[:, at + WINDOW:STEP_W], qkv[:, g, QW:QW + KW], cv("ident")[:, T * j:T * j + T],
                                            start=True, stop=True)
                if m >= 2:
                    pe.wait_ge(a_exp, HH * (m - 1))
                    for h in range(HH):
                        last = nc.tensor.transpose(ps[:, WINDOW * h:WINDOW * h + WINDOW], Pr[:, (m - 2) % 8, h, 0:WINDOW],
                                                   cv("ident"))
                last.then_inc(p_step, 1)

            def scores(n):
                g, j = divmod(n, BT)
                pe.wait_ge(a_step, n + 1)
                if j == 0:
                    pe.wait_ge(v_qbd, g + 1)
                if n == 0:
                    pe.wait_ge(s_mask, 32)
                    pe.wait_ge(v_dyn, 1)
                if n >= 2:
                    pe.wait_ge(a_exp, HH * (n - 1))
                for h in range(HH):
                    nc.tensor.matmul(S_ps[n % 2][:, h, :], sel_sb[:, n, :], maskr[:], start=True, stop=False)
                    last = nc.tensor.matmul(S_ps[n % 2][:, h, :], qbd[:, g % 2, BT * h + j, :, :].rearrange("p g t -> p (g t)"),
                                            ring[:, (n - 2) % 8, HH * WINDOW:STEP_W], start=False, stop=True)
                last.then_inc(p_s, 1)

            def probs_new_in(g):
                if g >= 1:
                    pe.wait_ge(a_ptn, g)
                else:
                    pe.wait_ge(a_kv, TILES)
                for h in range(HH):
                    for j in range(BT):
                        nc.tensor.matmul(PTn_ps[T * j:T * j + T, h, :], Pr[:, (BT * g + j) % 8, h, WINDOW:KEYS], cv("ident"),
                                         start=True, stop=True)
                pe.wait_ge(v_rdiag, g + 1)
                nc.tensor.matmul(rsum_ps, cv("group"), rdiag[:, g % 2, :, :].rearrange("p n t -> p (n t)"),
                                 start=True, stop=True).then_inc(p_ptn, 1)

            def values(n):
                g, j = divmod(n, BT)
                pe.wait_ge(a_step, n + 5)
                if j == 0:
                    pe.wait_ge(a_ptn, g + 1)
                    pe.wait_ge(v_vbd, g + 1)
                    if g >= 1:
                        pe.wait_ge(v_o, g)
                for part in range(2):
                    for k in range(G):
                        rows = slice(HD * k, HD * k + HD)
                        cols = slice(T * k, T * k + T)
                        if part == 0:
                            nc.tensor.matmul(O_ps[rows, j], hist[:, n, KW + HD * k:KW + HD * k + HD],
                                             free(ring[:, (n + 2) % 8, cols], (WINDOW, HH), (1, T)),
                                             start=True, stop=False)
                        else:
                            last = nc.tensor.matmul(O_ps[rows, j], Vbd[:, g % 2, j, rows], PTn_v[:, g % 2, :, cols],
                                                    start=False, stop=True)
                last.then_inc(p_o, 1)

            def rows_out(g):
                if g >= 1:
                    pe.wait_ge(v_res, g)
                pe.wait_ge(v_o, g + 1)
                for h in range(HH):
                    last = nc.tensor.matmul(res_ps, oT[:, g % 2, h, :, :].rearrange("p b t -> p (b t)"), Wo_sb[:, h, :],
                                            start=(h == 0), stop=(h == HH - 1))
                last.then_inc(p_res, 1)

            PTn_v = PTn[:, :, 0:HH * P].rearrange("p i (h k) -> p i h k", h=HH)
            queries_in(0)
            step_in(-2)
            step_in(-1)
            pe.wait_ge(s_wo, 16)
            for n in range(B + 7):
                g, k = divmod(n, BT)
                if n < B:
                    scores(n)
                if n < B + 2:
                    step_in(n)
                if k == 1 and g + 1 < TILES:
                    queries_in(g + 1)
                if k == 1 and 1 <= g <= TILES:
                    probs_new_in(g - 1)
                if 6 <= n < B + 6:
                    values(n - 6)
                if k == 2 and n >= 10:
                    rows_out((n - 10) // BT)


def kernel(**inputs):
    import concourse.bacc as bacc
    from concourse.bass_utils import run_bass_kernel_spmd

    a = {k: np.asarray(v) for k, v in inputs.items()}
    lens = a["itok_B_37_3939"]

    def heads_last(w):
        return w.reshape(G, HH, HD, D).transpose(3, 1, 0, 2).reshape(D, QW)

    def by_position(blocks):
        return blocks.transpose(0, 2, 1, 3).reshape(-1, KW)

    def over_partitions(w):
        return w.reshape(C, P, -1).transpose(1, 0, 2).reshape(P, -1)

    def every(v):
        return np.tile(v[None], (P, 1))

    band, select = mask_constants()
    per_batch = [np.tile(v.reshape(B, -1), (P // B, 1)) for v in (
        lens, a["itok_B_0_7"], a["itok_B_1_198"], a["itok_Bx257_0_4111"])]
    arrays = {
        "ints": np.concatenate([every(lens), np.repeat(lens.reshape(TILES, BT).T, T, 0), *per_batch[:3],
                                every(a["itok_B_0_3"]), per_batch[3]], axis=1),
        "const": np.concatenate([constants()[:, :CONST["q_scale"][0]], every(a["L3_cond_q_norm_scale"]),
                                 every(a["L3_cond_k_norm_scale"]),
                                 np.tile(np.repeat(a["L0_cond_scaling"], R), P // ER)[:, None]], axis=1),
        "low": np.concatenate([over_partitions(w) for w in (
            a["L0_cond_Wt"], a["L0_cond_A"].reshape(ER, D).T,
            a["L0_cond_B_w"].transpose(1, 0, 2).reshape(D, ER), a["L0_cond_Wp"].T)], axis=1),
        "xT": over_partitions(a["x"].reshape(TOK, D).T),
        "WbT": over_partitions(a["L0_cond_W_base"].T),
        "W1T": a["L1_cond_weights"].transpose(0, 2, 1).reshape(-1, T * T),
        "W2": a["L2_cond_weights"].reshape(-1, T * T),
        "WqkvT": over_partitions(np.concatenate(
            [heads_last(a["L3_cond_Wq"]), a["L3_cond_Wk"].T, a["L3_cond_Wv"].T], axis=1)),
        "WoT": over_partitions(a["L3_cond_Wo"].reshape(D, G, HH, HD).transpose(2, 1, 3, 0).reshape(D, D)),
        "cache": np.concatenate([by_position(a["L3_cond_k_blocks"]), by_position(a["L3_cond_v_blocks"])], axis=1),
        "band": band,
        "select": select,
    }
    arrays = {k: np.ascontiguousarray(v) for k, v in arrays.items()}
    nc = bacc.Bacc("TRN2", target_bir_lowering=False, num_devices=1)
    args = [nc.dram_tensor(k, v.shape, mybir.dt.from_np(v.dtype), kind="ExternalInput").ap() for k, v in arrays.items()]
    for name, shape in (("new_rows", [TOK, 2 * KW]), ("w1_rows", [B, T * T]), ("w2_rows", [B, T * T])):
        args.append(nc.dram_tensor(name, shape, F32, kind="Internal").ap())
    args.append(nc.dram_tensor("out", [TOK, D], F32, kind="ExternalOutput").ap())
    cond_resid_kernel(nc, *args)
    got = run_bass_kernel_spmd(nc, [arrays], core_ids=[0])
    return got.results[0]["out"].reshape(B, T, D)
```

```python
from contextlib import ExitStack

import concourse.bass as bass
import numpy as np
from concourse import mybir

ALU = mybir.AluOpType
ACT = mybir.ActivationFunctionType
F32 = mybir.dt.float32
BF16 = mybir.dt.bfloat16
I32 = mybir.dt.int32
U32 = mybir.dt.uint32
U16 = mybir.dt.uint16
AX_X = mybir.AxisListType.X

B, T, D = 32, 32, 256
P = 128
BT = P // T
TILES = B // BT
TOK = B * T
C = D // P
E, R = 4, 16
ER = E * R
G, HH, HD = 4, 2, 32
HALF = HD // 2
KW = G * HD
QW = HH * KW
HEADS = G * HH + G
WINDOW = 128
BLOCK = 16
SLOTS = 257
LOOK = 12
BACK = WINDOW // BLOCK
RUNS = 3
NCOL = B + TILES
COLS_AT_ONCE = NCOL // 4
KEYS = WINDOW + T
STEP_W = HH * WINDOW + WINDOW
EPS = 1e-6
SCALE = float(D) ** -0.5
MASKED = -1e30
BIAS = float(1 << 17)
NONE = float(1 << 20)
MAGIC = 12582912.0
TWO_PI = (6.28125, 0.0019350051879882812, 3.019916050561552e-07)
PI_SAFE = 3.1415925
AHEAD = 20
FIRST, EACH = 16, 3
LATE = [9 + 5 * j // 3 for j in range(B - AHEAD)]

CONST = {}
_at = 0
for _name, _n in (("ident", P), ("slot", SLOTS), ("look", LOOK), ("target", 3), ("offset", NCOL),
                  ("t", 1), ("inv", HALF), ("same", P), ("pick", 4 * TILES), ("adapter", 1),
                  ("order", RUNS * B), ("key", WINDOW), ("group", P), ("t_eye", T),
                  ("q_scale", HD), ("k_scale", HD), ("scaling", 1)):
    CONST[_name] = (_at, _n)
    _at += _n
CONST_W = _at

INTS = {"lens_col": (0, NCOL), "lens_rb": (NCOL, 1), "w1_idx": (NCOL + 1, 1), "w2_idx": (NCOL + 2, 1),
        "adapter_idx": (NCOL + 3, B), "table": (NCOL + 3 + B, SLOTS)}
INTS_W = NCOL + 3 + B + SLOTS
LOW = {"Wt": (0, D), "AT": (C * D, ER), "Bo": (C * (D + ER), ER), "WpT": (C * (D + 2 * ER), D)}
LOW_W = C * (2 * D + 2 * ER)


def constants():
    p = np.arange(P)
    c = np.zeros((P, CONST_W), np.float32)

    def put(name, v):
        a, n = CONST[name]
        c[:, a:a + n] = v

    put("ident", np.eye(P))
    put("slot", np.arange(SLOTS)[None])
    put("look", np.arange(LOOK)[None])
    put("target", (p // B)[:, None] + 4 * np.arange(3)[None] - BACK)
    put("offset", np.concatenate([np.repeat(p[:, None], B, 1), np.repeat(WINDOW + p[:, None] % T, TILES, 1)], 1))
    put("t", (p % T)[:, None])
    put("inv", (np.float32(1.0) / np.float32(10000.0) ** (np.arange(HALF, dtype=np.float32) / np.float32(HALF)))[None])
    put("same", ((p[:, None] % B) % BT == p[None] // T))
    rb = np.arange(4 * TILES)
    put("pick", (p[:, None] // B == rb[None] // TILES) & ((p[:, None] % B) // BT == rb[None] % TILES))
    put("adapter", (p // R)[:, None])
    i, b = np.arange(RUNS * B) // B, np.arange(RUNS * B) % B
    put("order", (T * b + BLOCK * i)[None] + BIAS - 0.5)
    put("key", np.arange(WINDOW)[None])
    put("group", p[:, None] // HD == p[None] // HD)
    put("t_eye", p[:, None] % T == np.arange(T)[None])
    return c


def mask_constants():
    t, key = np.arange(T)[:, None], np.arange(KEYS)[None]
    band = np.where((key > t) & (key <= t + WINDOW), 0.0, MASKED)
    sel = np.zeros((2, 32, B, G, T))
    sel[0] = np.eye(T)[:, None, None, :]
    sel[1] = np.eye(B)[:, :, None, None]
    return [(v.astype(np.float32).view(np.uint32) >> 16).astype(np.uint16) for v in (band, sel.reshape(64, B * P))]


def free(ap, *dims):
    return bass.AP(tensor=ap.tensor, offset=ap.offset, ap=[list(ap.ap[0])] + [list(d) for d in dims])


def dram(ap, *dims):
    return bass.AP(tensor=ap.tensor, offset=ap.offset, ap=[list(d) for d in dims])


def cond_resid_kernel(nc, ints, const, low, xT, WbT, W1T, W2, WqkvT, WoT, cache, band, select,
                      new_rows, w1_rows, w2_rows, out):
    with ExitStack() as ctx:
        def sb(name, shape, dt=F32):
            return ctx.enter_context(nc.sbuf_tensor(name, shape, dt))

        def sem(name):
            return ctx.enter_context(nc.semaphore(name))

        bank = [ctx.enter_context(nc.psum_tensor(f"bank{i}", [P, 512], F32)) for i in range(8)]

        cst = sb("cst", [P, CONST_W])
        ints_sb = sb("ints_sb", [P, INTS_W], I32)
        low_sb = sb("low_sb", [P, LOW_W])
        lens_dyn = sb("lens_dyn", [64, 1])
        xT_sb = sb("xT_sb", [P, C, TOK])
        Wb_sb = sb("Wb_sb", [P, C, D])
        Wqkv_sb = sb("Wqkv_sb", [P, C, QW + 2 * KW])
        Wo_sb = sb("Wo_sb", [P, HH, D])
        maskr = sb("maskr", [P, KEYS], BF16)
        sel_sb = sb("sel_sb", [P, B, P], BF16)

        slot0 = sb("slot0", [P, 1], I32)
        target = sb("target", [P, 3])
        junk = sb("junk", [P, 3, SLOTS])
        looked = sb("looked", [P, 3])
        look_all = sb("look_all", [P, 3, P])
        look_own = sb("look_own", [P, 3, 4 * TILES])
        ones = sb("ones", [P, P])
        eps = sb("eps", [P, 1])
        inblk = sb("inblk", [P, NCOL], I32)
        place = sb("place", [P, NCOL], I32)
        slot_of = sb("slot_of", [P, NCOL], I32)
        off_of = sb("off_of", [P, NCOL], I32)
        hit = sb("hit", [P, LOOK, NCOL])
        block_of = sb("block_of", [P, NCOL])
        row_of = sb("row_of", [P, NCOL])
        hist_idx = sb("hist_idx", [P, B], I32)
        run_lo = sb("run_lo", [P, RUNS, B])
        run_hi = sb("run_hi", [P, RUNS, B])
        run_shift = sb("run_shift", [P, RUNS, B])
        run_sum = sb("run_sum", [P, RUNS * B])
        run_len = sb("run_len", [P, RUNS * B])
        run_reach = sb("run_reach", [P, RUNS * B])
        best = sb("best", [P, NCOL])
        nobody = sb("nobody", [P, NCOL])
        patch_idx = sb("patch_idx", [P, NCOL], I32)

        pos = sb("pos", [P, TILES])
        ang = sb("ang", [P, TILES, 2, HALF])
        turns = sb("turns", [P, TILES, 2, HALF])
        cossin = sb("cossin", [P, TILES, 2, HALF])
        plus1 = sb("plus1", [P, 2, HD])
        cross1 = sb("cross1", [P, 2, HD])
        rot_same = sb("rot_same", [P, TILES, 2, HD])
        rot_cross = sb("rot_cross", [P, TILES, 2, HD])

        mask0 = sb("mask0", [ER, B])
        AW_sb = sb("AW_sb", [P, C, ER])
        C_sb = sb("C_sb", [ER, D])
        zm = sb("zm", [ER, TOK])
        w1_sb = sb("w1_sb", [B, T * T])
        w2_sb = sb("w2_sb", [B, T * T])
        bd1 = sb("bd1", [P, TILES, P])
        bd2 = sb("bd2", [P, TILES, P])
        M_sb = sb("M_sb", [P, TILES, P])
        x1 = sb("x1", [P, TILES, D])
        x3T = sb("x3T", [P, TILES, C, P])

        qkv = sb("qkv", [P, TILES, QW + 2 * KW])
        sq = sb("sq", [P, TILES, QW])
        ssum = sb("ssum", [P, TILES, HEADS])
        root = sb("root", [P, TILES, HEADS])
        rnorm = sb("rnorm", [P, TILES, HEADS])
        normed = sb("normed", [P, 2 * QW])
        same = sb("same", [P, 2 * QW])
        cross = sb("cross", [P, 2 * QW])
        unread = sb("unread", [P, 1])
        hist = sb("hist", [P, B, 2 * KW])
        qbd = sb("qbd", [P, 2, HH * BT, G, T])
        negmax = sb("negmax", [P, 4, HH])
        esum = sb("esum", [P, 2, BT * HH])
        rsum = sb("rsum", [P, BT * HH])
        rdiag = sb("rdiag", [P, 2, BT * HH, T])
        shared = sb("shared", [P, 8 * (HH * KEYS + STEP_W + T)])
        Pr = shared[:, 0:8 * HH * KEYS].rearrange("p (n h k) -> p n h k", n=8, h=HH)
        ring = shared[:, 8 * HH * KEYS:].rearrange("p (n k) -> p n k", n=8)
        above = shared[:, 0:NCOL * RUNS * B].rearrange("p (n j) -> p n j", n=NCOL)
        Pr_new = sb("Pr_new", [P, 2, HH, BT, T])
        PTbd = sb("PTbd", [P, 2, G, BT, HH, T])
        rsum_wide = sb("rsum_wide", [P, 2, BT * HH * T])
        oT = sb("oT", [P, 2, HH, BT, T])
        res = sb("res", [P, 2, D])

        def cv(name, rows=slice(0, P)):
            a, n = CONST[name]
            return cst[rows, a:a + n]

        def iv(name, rows=slice(0, P)):
            a, n = INTS[name]
            return ints_sb[rows, a:a + n]

        def lv(name):
            a, n = LOW[name]
            return low_sb[:, a:a + C * n].rearrange("p (c n) -> p c n", c=C)

        s_int, s_cst, s_low, s_x, s_wb, s_qkvw, s_wo, s_mask = map(sem, (
            "s_int", "s_cst", "s_low", "s_x", "s_wb", "s_qkvw", "s_wo", "s_mask"))
        s_w1g, s_w2g, s_w1d, s_w2d, s_bd1, s_bd2 = map(sem, ("s_w1g", "s_w2g", "s_w1d", "s_w2d", "s_bd1", "s_bd2"))
        s_new = sem("s_new")
        s_hist = [sem(f"s_hist{b}") for b in range(B)]
        s_own = [sem(f"s_own{g}") for g in range(TILES)]
        s_patch = [sem(f"s_patch{b}") for b in range(B)]
        s_out = [sem(f"s_out{g}") for g in range(2)]
        z_bd, z_misc = sem("z_bd"), sem("z_misc")
        v_chain = sem("v_chain")
        g_chain, g_ang, g_rot, g_B2, g_run = map(sem, ("g_chain", "g_ang", "g_rot", "g_B2", "g_run"))
        v_look, v_ang, v_idx, v_run, v_patch, v_wb, v_zm, v_scale, v_M, v_dyn = map(sem, (
            "v_look", "v_ang", "v_idx", "v_run", "v_patch", "v_wb", "v_zm", "v_scale", "v_M", "v_dyn"))
        v_ksum, v_k, v_qsum, v_q, v_max, v_kn, v_qbd, v_new, v_ptn, v_rdiag, v_rsum, v_o, v_res = map(sem, (
            "v_ksum", "v_k", "v_qsum", "v_q", "v_max", "v_kn", "v_qbd", "v_new", "v_ptn", "v_rdiag", "v_rsum", "v_o", "v_res"))
        a_AW, a_C, a_x1, a_x3T, a_x3, a_kv, a_ksq, a_kroot, a_qraw, a_qsq, a_qroot, a_sin, a_near = map(sem, (
            "a_AW", "a_C", "a_x1", "a_x3T", "a_x3", "a_kv", "a_ksq", "a_kroot", "a_qraw", "a_qsq", "a_qroot", "a_sin", "a_near"))
        a_exp, a_qbd, a_step, a_ptn = map(sem, ("a_exp", "a_qbd", "a_step", "a_ptn"))
        p_look, p_AW, p_C, p_z, p_x1, p_M, p_x3T, p_x3, p_kv, p_qraw = map(sem, (
            "p_look", "p_AW", "p_C", "p_z", "p_x1", "p_M", "p_x3T", "p_x3", "p_kv", "p_qraw"))
        p_qT, p_kn, p_s, p_step, p_ptn, p_o, p_res = map(sem, ("p_qT", "p_kn", "p_s", "p_step", "p_ptn", "p_o", "p_res"))

        looked_ps = bank[0][:, 0:LOOK * NCOL].rearrange("p (j n) -> p j n", j=LOOK)
        AW_ps = bank[1][:, 0:C * ER].rearrange("p (c n) -> p c n", c=C)
        C_ps = bank[2][0:ER, 0:D]
        z_ps = [bank[3], bank[4]]
        x1_ps = [bank[5][:, 0:D], bank[6][:, 0:D], bank[7][:, 0:D]]
        M_ps = [bank[1][:, :].rearrange("p (i n) -> p i n", i=4), bank[2][:, :].rearrange("p (i n) -> p i n", i=4)]
        x3T_ps = [bank[3][:, 0:D].rearrange("p (c n) -> p c n", c=C), bank[4][:, 0:D].rearrange("p (c n) -> p c n", c=C)]
        x3_ps = [bank[3][:, 0:D], bank[4][:, 0:D]]
        kv_ps = [bank[i][:, 0:2 * KW] for i in (5, 6, 7)]
        q_ps = [bank[i][:, 0:QW] for i in (0, 1, 2)]

        S_ps = [bank[i][:, 0:HH * KEYS].rearrange("p (h k) -> p h k", h=HH) for i in (0, 1)]
        qT_ps = bank[2][:, 0:HH * P].rearrange("p (h k) -> p h k", h=HH)
        step_ps = [bank[3][:, 0:STEP_W], bank[4][:, 0:STEP_W]]
        PTn_ps = bank[5][:, 0:HH * P].rearrange("p (h k) -> p h k", h=HH)

        def PTn_by_head(rows):
            return PTn_ps[rows].rearrange("p h (g t) -> p g h t", g=G)

        rsum_ps = bank[5][:, HH * P:2 * HH * P]
        O_ps = bank[6][:, 0:BT * HH * T].rearrange("p (b h t) -> p b h t", b=BT, h=HH)
        res_ps = [bank[7][:, 0:D]] * (TILES - 1) + [bank[0][:, 0:D]]
        kn_ps = bank[7][:, D:D + P]

        block = ctx.enter_context(nc.Block())

        @block.sync
        def _(sp):
            sp.dma_start(ints_sb[:], ints).then_inc(s_int, 16)
            sp.dma_start(low_sb[:], low).then_inc(s_low, 16)
            sp.dma_start(Wb_sb[:], WbT.rearrange("p (c n) -> p c n", c=C)).then_inc(s_wb, 16)
            for got, gathered, rows, wrote in ((s_w1g, w1_sb, w1_rows, s_w1d), (s_w2g, w2_sb, w2_rows, s_w2d)):
                sp.wait_ge(got, 16)
                sp.dma_start(rows, gathered[:]).then_inc(wrote, 16)
            sp.wait_ge(z_bd, 2)
            for rows, wrote, bd, done in ((w2_rows, s_w2d, bd2, s_bd2), (w1_rows, s_w1d, bd1, s_bd1)):
                sp.wait_ge(wrote, 16)
                for j in range(BT):
                    src = rows.rearrange("(n j) (k c) -> j k n c", j=BT, k=T)[j]
                    sp.dma_start(bd[T * j:T * j + T, :, T * j:T * j + T], src).then_inc(done, 16)
            sp.dma_start(Wo_sb[:], WoT.rearrange("p (h n) -> p h n", h=HH)).then_inc(s_wo, 16)
            new_tiles = new_rows.rearrange("(i p) n -> p i n", p=P)
            for j in range(TILES // 2):
                sp.wait_ge(v_k, j + 1)
                sp.wait_ge(a_kv, 2 * j + 2)
                sp.dma_start(new_tiles[:, 2 * j:2 * j + 2, :], qkv[:, 2 * j:2 * j + 2, QW:]).then_inc(s_new, 16)
            for i in range(TILES):
                sp.wait_ge(v_res, i + 1)
                sp.dma_start(out[P * i:P * i + P, :], res[:, i % 2, :]).then_inc(s_out[i % 2], 16)
            sp.wait_ge(s_out[0], 16 * (TILES // 2))
            sp.wait_ge(s_out[1], 16 * (TILES // 2))

        @block.gpsimd
        def _(pool):
            count = [0]

            def link(ins):
                count[0] += 1
                ins.then_inc(g_chain, 1)
                pool.wait_ge(g_chain, count[0])

            nc.gpsimd.memset(bd1[:], 0.0).then_inc(z_bd, 1)
            nc.gpsimd.memset(bd2[:], 0.0).then_inc(z_bd, 1)
            pool.wait_ge(s_int, 16)
            for rows, table, name, got in ((w1_sb, W1T, "w1_idx", s_w1g), (w2_sb, W2, "w2_idx", s_w2g)):
                nc.gpsimd.indirect_dma_start(
                    rows[:], None, table,
                    bass.IndirectOffsetOnAxis(ap=iv(name, slice(0, B)).bitcast(U32), axis=0)).then_inc(got, 16)

            pool.wait_ge(s_cst, 16)
            link(nc.gpsimd.tensor_scalar(pos[:], iv("lens_col")[:, B:NCOL], cv("t"), None, ALU.add))
            link(nc.gpsimd.tensor_tensor(ang[:], free(pos[:], (1, TILES), (0, 2), (0, HALF)),
                                         free(cv("inv"), (0, TILES), (0, 2), (1, HALF)), ALU.mult))
            nc.gpsimd.tensor_scalar(turns[:, :, 0, :], ang[:, :, 0, :], 1.0 / (2.0 * np.pi), 0.25, ALU.mult,
                                    ALU.add).then_inc(g_ang, 1)
            nc.gpsimd.tensor_scalar(turns[:, :, 1, :], ang[:, :, 1, :], 1.0 / (2.0 * np.pi), None,
                                    ALU.mult).then_inc(g_ang, 1)

            def gather(b):
                nc.gpsimd.indirect_dma_start(
                    hist[:, b, :], None, cache,
                    bass.IndirectOffsetOnAxis(ap=hist_idx[:, b:b + 1].bitcast(U32), axis=0)).then_inc(s_hist[b], 16)

            def within(part):
                pool.wait_ge(a_near, COLS_AT_ONCE * (part + 1))
                pool.wait_ge(v_run, 2)
                to_all = above[:, COLS_AT_ONCE * part:COLS_AT_ONCE * (part + 1), :]
                nc.gpsimd.tensor_tensor(to_all, free(run_reach[:], (0, COLS_AT_ONCE), (1, RUNS * B)), to_all,
                                        ALU.subtract).then_inc(g_run, 1)

            def patch(i):
                nc.gpsimd.indirect_dma_start(
                    qkv[:, i, QW:], None, new_rows,
                    bass.IndirectOffsetOnAxis(ap=patch_idx[:, B + i:B + i + 1].bitcast(U32), axis=0),
                    bounds_check=TOK - 1, oob_is_err=False).then_inc(s_own[i], 16)
                for b in range(BT * i, BT * i + BT):
                    pool.wait_ge(s_hist[b], 16)
                    nc.gpsimd.indirect_dma_start(
                        hist[:, b, :], None, new_rows,
                        bass.IndirectOffsetOnAxis(ap=patch_idx[:, b:b + 1].bitcast(U32), axis=0),
                        bounds_check=TOK - 1, oob_is_err=False).then_inc(s_patch[b], 16)
                    if b in LATE:
                        gather(AHEAD + LATE.index(b))

            pool.wait_ge(g_ang, 2)
            nc.gpsimd.memset(sel_sb[64:P, :, :].bitcast(F32), 0.0).then_inc(z_misc, 1)
            pool.wait_ge(z_misc, 1)
            nc.gpsimd.memset(maskr[:].bitcast(F32), 0.0).then_inc(z_misc, 1)
            nc.gpsimd.memset(qbd[:], 0.0).then_inc(z_misc, 1)
            nc.gpsimd.memset(PTbd[:], 0.0).then_inc(z_misc, 1)
            pool.wait_ge(v_idx, 1)
            for b in range(BT):
                gather(b)
            within(0)
            pool.wait_ge(s_bd2, 16 * BT)
            nc.gpsimd.tensor_tensor(bd2[:], bd2[:], free(cv("ident"), (0, TILES), (1, P)), ALU.add).then_inc(g_B2, 1)
            within(1)
            pool.wait_ge(v_scale, 1)
            pool.wait_ge(a_sin, 1)
            for w in range(2):
                for table, scale, fn in ((rot_same, plus1, 0), (rot_cross, cross1, 1)):
                    nc.gpsimd.tensor_tensor(free(table[:, 0, w, :], (2 * HD, TILES), (HALF, 2), (1, HALF)),
                                            free(cossin[:, 0, fn, :], (2 * HALF, TILES), (0, 2), (1, HALF)),
                                            free(scale[:, w, :], (0, TILES), (HALF, 2), (1, HALF)), ALU.mult).then_inc(g_rot, 1)
            within(2)
            within(3)
            for b in range(BT, AHEAD):
                gather(b)
            pool.wait_ge(v_patch, 1)
            pool.wait_ge(s_new, 16 * (TILES // 2))
            for i in range(TILES):
                patch(i)

        @block.scalar
        def _(act):
            act.dma_start(cst[:], const).then_inc(s_cst, 16)
            act.dma_start(xT_sb[:], xT.rearrange("p (c n) -> p c n", c=C)).then_inc(s_x, 16)
            act.dma_start(Wqkv_sb[:], WqkvT.rearrange("p (c n) -> p c n", c=C)).then_inc(s_qkvw, 16)

            act.wait_ge(p_AW, 1)
            nc.scalar.copy(AW_sb[:], AW_ps).then_inc(a_AW, 1)
            act.wait_ge(p_C, 1)
            nc.scalar.copy(C_sb[:], C_ps).then_inc(a_C, 1)
            act.wait_ge(v_ang, 1)
            nc.scalar.activation(cossin[:], ang[:], ACT.Sin).then_inc(a_sin, 1)
            act.wait_ge(v_run, 1)
            nc.scalar.activation(unread[:], eps[:], ACT.Sqrt)
            def distances(cols):
                for c in cols:
                    nc.scalar.activation(above[:, c, :], run_sum[:], ACT.Square, scale=-0.5,
                                         bias=row_of[:, c:c + 1]).then_inc(a_near, 1)

            distances(range(FIRST))
            for i in range(TILES):
                act.wait_ge(p_x1, i + 1)
                nc.scalar.copy(x1[:, i, :], x1_ps[i % 3]).then_inc(a_x1, 1)
                distances(range(FIRST + EACH * i, min(FIRST + EACH * (i + 1), NCOL)))

            def k_root(j):
                act.wait_ge(v_ksum, j + 1)
                nc.scalar.activation(root[:, 2 * j:2 * j + 2, HH * G:HEADS], ssum[:, 2 * j:2 * j + 2, HH * G:HEADS],
                                     ACT.Sqrt, scale=1.0 / HD, bias=eps[:, 0:1]).then_inc(a_kroot, 1)

            for i in range(TILES + 1):
                if i < TILES:
                    act.wait_ge(p_x3T, i + 1)
                    nc.scalar.copy(x3T[:, i, :, :], x3T_ps[i % 2]).then_inc(a_x3T, 1)
                if i >= 1:
                    j = i - 1
                    act.wait_ge(p_kv, i)
                    nc.scalar.copy(qkv[:, j, QW:], kv_ps[j % 3]).then_inc(a_kv, 1)
                    act.wait_ge(a_kv, i)
                    nc.scalar.activation(sq[:, j, 0:KW], qkv[:, j, QW:QW + KW], ACT.Square).then_inc(a_ksq, 1)
                    if j >= 3 and j % 2 == 1:
                        k_root(j // 2 - 1)
            act.wait_ge(z_misc, 4)
            act.dma_start(sel_sb[0:64, :, :].bitcast(U16), select.rearrange("p (b n) -> p b n", b=B)).then_inc(s_mask, 16)
            act.dma_start(maskr[0:T, :].bitcast(U16), band).then_inc(s_mask, 16)
            def q_root(j):
                act.wait_ge(v_qsum, j + 1)
                nc.scalar.activation(root[:, 2 * j:2 * j + 2, 0:HH * G], ssum[:, 2 * j:2 * j + 2, 0:HH * G],
                                     ACT.Sqrt, scale=1.0 / HD, bias=eps[:, 0:1]).then_inc(a_qroot, 1)

            for j in range(TILES):
                act.wait_ge(p_qraw, j + 1)
                nc.scalar.copy(qkv[:, j, 0:QW], q_ps[j % 3]).then_inc(a_qraw, 1)
                if j == 0:
                    k_root(TILES // 2 - 1)
                act.wait_ge(a_qraw, j + 1)
                nc.scalar.activation(sq[:, j, :], qkv[:, j, 0:QW], ACT.Square).then_inc(a_qsq, 1)
                act.wait_ge(p_x3, j + 1)
                nc.scalar.copy(x1[:, j, :], x3_ps[j % 2]).then_inc(a_x3, 1)
                if j == 3:
                    q_root(0)
            q_root(1)

            def step_out(m):
                act.wait_ge(p_step, m + 3)
                if m >= 6:
                    act.wait_ge(p_s, m - 5)
                if m >= 10:
                    act.wait_ge(p_o, m - 9)
                cols = slice(0 if m >= 2 else HH * WINDOW, STEP_W if m + 2 < B else HH * WINDOW)
                nc.scalar.copy(ring[:, (m + 2) % 8, cols], step_ps[m % 2][:, cols]).then_inc(a_step, 1)

            def exps(n):
                g, j = divmod(n, BT)
                act.wait_ge(v_max, n + 1)
                if n >= 8:
                    act.wait_ge(p_step, n - 3)
                    act.wait_ge(v_new, g - 1)
                    act.wait_ge(v_rdiag, g - 1)
                for h in range(HH):
                    nc.scalar.activation(Pr[:, n % 8, h, :], S_ps[n % 2][:, h, :], ACT.Exp, bias=negmax[:, n % 4, h:h + 1],
                                         accum_out=esum[:, g % 2, HH * j + h:HH * j + h + 1]).then_inc(a_exp, 1)

            def qbd_out(g):
                act.wait_ge(p_qT, g + 1)
                if g >= 2:
                    act.wait_ge(p_s, BT * (g - 1))
                if g == 0:
                    act.wait_ge(z_misc, 4)
                for j in range(G // 2, G):
                    rows = slice(HD * j, HD * j + HD)
                    last = nc.scalar.copy(qbd[rows, g % 2, :, j, :],
                                          bank[2][rows, 0:HH * P].rearrange("p (n t) -> p n t", t=T))
                last.then_inc(a_qbd, 1)

            def new_probs_out(g):
                act.wait_ge(p_ptn, g + 1)
                if g >= 2:
                    act.wait_ge(p_o, BT * (g - 1))
                    act.wait_ge(v_o, g - 1)
                nc.scalar.copy(rsum_wide[P // 2:, g % 2, :], rsum_ps[P // 2:])
                for j in range(BT // 2, BT):
                    rows = slice(T * j, T * j + T)
                    last = nc.scalar.copy(PTbd[rows, g % 2, :, j, :, :], PTn_by_head(rows))
                last.then_inc(a_ptn, 1)

            qbd_out(0)
            q_root(2)
            q_root(3)
            step_out(-2)
            step_out(-1)
            nc.scalar.activation(unread[:], eps[:], ACT.Exp)
            for n in range(B + 7):
                g, k = divmod(n, BT)
                if n < B:
                    exps(n)
                if n < B + 2:
                    step_out(n)
                if k == 2 and 1 <= g <= TILES:
                    new_probs_out(g - 1)
                if k == 2 and g + 1 < TILES:
                    qbd_out(g + 1)

        @block.vector
        def _(dve):
            count = [0]

            def link(ins):
                count[0] += 1
                ins.then_inc(v_chain, 1)
                dve.wait_ge(v_chain, count[0])

            nc.vector.memset(eps[:], EPS)
            link(nc.vector.memset(ones[:], 1.0))
            dve.wait_ge(s_int, 16)
            link(nc.vector.tensor_single_scalar(slot0[:], iv("lens_rb"), 4, ALU.arith_shift_right))
            dve.wait_ge(s_cst, 16)
            link(nc.vector.tensor_scalar(target[:], cv("target"), slot0[:, 0:1], None, ALU.add))
            for m in range(3):
                last = nc.vector.scalar_tensor_tensor(out=junk[:, m, :], in0=cv("slot"), scalar=target[:, m:m + 1],
                                                      in1=iv("table"), op0=ALU.is_equal, op1=ALU.mult,
                                                      accum_out=looked[:, m:m + 1])
            link(last)
            nc.vector.tensor_tensor(look_all[:], free(cv("ident"), (0, 3), (1, P)), free(looked[:], (1, 3), (0, P)),
                                    ALU.mult).then_inc(v_look, 1)
            nc.vector.tensor_tensor(look_own[:], free(cv("pick"), (0, 3), (1, 4 * TILES)),
                                    free(looked[:], (1, 3), (0, 4 * TILES)), ALU.mult).then_inc(v_look, 1)
            link(nc.vector.tensor_single_scalar(inblk[:], iv("lens_col"), BLOCK - 1, ALU.bitwise_and))
            link(nc.vector.tensor_tensor(place[:], inblk[:], cv("offset"), ALU.add))
            nc.vector.tensor_single_scalar(slot_of[:], place[:], 4, ALU.arith_shift_right)
            link(nc.vector.tensor_single_scalar(off_of[:], place[:], BLOCK - 1, ALU.bitwise_and))
            link(nc.vector.tensor_tensor(hit[:], free(cv("look"), (1, LOOK), (0, NCOL)),
                                         free(slot_of[:], (0, LOOK), (1, NCOL)), ALU.is_equal))
            dve.wait_ge(g_ang, 2)
            link(nc.vector.tensor_scalar(turns[:], turns[:], MAGIC, MAGIC, ALU.add, ALU.subtract))
            flat = "p n s d -> p (n s d)"
            for part in TWO_PI:
                link(nc.vector.scalar_tensor_tensor(out=ang[:].rearrange(flat), in0=turns[:].rearrange(flat), scalar=-part,
                                                    in1=ang[:].rearrange(flat), op0=ALU.mult, op1=ALU.add))
            link(nc.vector.tensor_scalar(ang[:, :, 0, :], ang[:, :, 0, :], float(np.pi / 2), None, ALU.add))
            nc.vector.tensor_scalar(ang[:], ang[:], PI_SAFE, -PI_SAFE, ALU.min, ALU.max).then_inc(v_ang, 1)
            nc.vector.tensor_scalar(plus1[:, 0, :], cv("q_scale"), 1.0, SCALE, ALU.add, ALU.mult)
            link(nc.vector.tensor_scalar(plus1[:, 1, :], cv("k_scale"), 1.0, None, ALU.add))
            nc.vector.tensor_copy(cross1[:, :, 0:HALF], plus1[:, :, 0:HALF])
            nc.vector.tensor_scalar(cross1[:, :, HALF:HD], plus1[:, :, HALF:HD], -1.0, None, ALU.mult).then_inc(v_scale, 1)
            dve.wait_ge(p_look, 1)
            link(nc.vector.tensor_tensor(hit[:], hit[:], looked_ps, ALU.mult))
            link(nc.vector.tensor_reduce(block_of[:], hit[:].rearrange("p j n -> p n j"), AX_X, ALU.add))
            link(nc.vector.scalar_tensor_tensor(out=row_of[:], in0=block_of[:], scalar=float(BLOCK), in1=off_of[:],
                                                op0=ALU.mult, op1=ALU.add))
            nc.vector.tensor_copy(hist_idx[:], row_of[:, 0:B]).then_inc(v_idx, 1)

            own = looked_ps[:, BACK:BACK + RUNS, 0:B]
            link(nc.vector.tensor_scalar(run_lo[:], own, float(BLOCK), -0.5, ALU.mult, ALU.add))
            nc.vector.tensor_scalar(run_hi[:], run_lo[:], float(BLOCK), None, ALU.add)
            link(nc.vector.scalar_tensor_tensor(out=run_shift[:].rearrange("p i b -> p (i b)"),
                                                in0=run_lo[:].rearrange("p i b -> p (i b)"), scalar=-1.0,
                                                in1=cv("order"), op0=ALU.mult, op1=ALU.add))
            nc.vector.tensor_tensor(run_shift[:], run_shift[:], free(inblk[:, 0:B], (0, RUNS), (1, B)), ALU.subtract)
            nc.vector.tensor_tensor(run_hi[:, 2, :], run_lo[:, 2, :], inblk[:, 0:B], ALU.add)
            link(nc.vector.tensor_tensor(run_lo[:, 0, :], run_lo[:, 0, :], inblk[:, 0:B], ALU.add))
            lo, hi = run_lo[:].rearrange("p i b -> p (i b)"), run_hi[:].rearrange("p i b -> p (i b)")
            nc.vector.tensor_tensor(run_sum[:], lo, hi, ALU.add).then_inc(v_run, 1)
            link(nc.vector.tensor_tensor(run_len[:], hi, lo, ALU.subtract))
            nc.vector.scalar_tensor_tensor(out=run_reach[:], in0=run_len[:], scalar=0.25, in1=run_len[:],
                                           op0=ALU.mult, op1=ALU.mult).then_inc(v_run, 1)

            dve.wait_ge(s_wb, 16)
            for c in range(C):
                w = Wb_sb[:, c, P * c:P * c + P]
                nc.vector.tensor_tensor(w, w, cv("ident"), ALU.add).then_inc(v_wb, 1)
            link(nc.vector.tensor_scalar(mask0[:], iv("adapter_idx", slice(0, ER)), cv("adapter", slice(0, ER)),
                                         cv("scaling", slice(0, ER)), ALU.is_equal, ALU.mult))
            for h in range(2):
                dve.wait_ge(p_z, h + 1)
                nc.vector.tensor_tensor(zm[:, 512 * h:512 * h + 512].rearrange("p (b t) -> p b t", t=T),
                                        z_ps[h][0:ER, :].rearrange("p (b t) -> p b t", t=T),
                                        free(mask0[:, 16 * h:16 * h + 16], (1, 16), (0, T)), ALU.mult).then_inc(v_zm, 1)

            def find(part):
                dve.wait_ge(g_run, part + 1)
                cols = slice(COLS_AT_ONCE * part, COLS_AT_ONCE * (part + 1))
                to_all = above[:, cols, :]
                link(nc.vector.scalar_tensor_tensor(
                    out=to_all, in0=to_all, scalar=0.0,
                    in1=free(run_shift[:], (0, COLS_AT_ONCE), (1, RUNS * B)), op0=ALU.is_gt, op1=ALU.mult))
                link(nc.vector.tensor_reduce(best[:, cols], to_all, AX_X, ALU.max))

            find(0)
            for h in range(2):
                dve.wait_ge(p_M, h + 1)
                nc.vector.tensor_tensor(M_sb[:, 4 * h:4 * h + 4, :], M_ps[h], bd2[:, 4 * h:4 * h + 4, :],
                                        ALU.add).then_inc(v_M, 1)
                find(1 + h)


            def rotate(w, heads, j, steps=range(4)):
                two, first, start = slice(2 * j, 2 * j + 2), HH * G * w, QW * w
                x = qkv[:, two, start:start + heads * HD].rearrange("p i (g d) -> p i g d", d=HD)
                n, s_, c_ = (v[:, 0:2 * heads * HD].rearrange("p (i g d) -> p i g d", i=2, d=HD)
                             for v in (normed, same, cross))
                for step in steps:
                    if step == 0:
                        link(nc.vector.reciprocal(rnorm[:, two, first:first + heads], root[:, two, first:first + heads]))
                        last = nc.vector.tensor_tensor(
                            n, x, free(rnorm[:, 2 * j, first:first + heads], (HEADS, 2), (1, heads), (0, HD)), ALU.mult)
                    elif step == 1:
                        last = nc.vector.tensor_tensor(
                            s_, n, free(rot_same[:, 2 * j, w, :], (2 * HD, 2), (0, heads), (1, HD)), ALU.mult)
                    elif step == 2:
                        last = nc.vector.tensor_tensor(
                            c_, n, free(rot_cross[:, 2 * j, w, :], (2 * HD, 2), (0, heads), (1, HD)), ALU.mult)
                    else:
                        nc.vector.tensor_tensor(x[:, :, :, 0:HALF], s_[:, :, :, 0:HALF], c_[:, :, :, HALF:HD], ALU.add)
                        last = nc.vector.tensor_tensor(x[:, :, :, HALF:HD], s_[:, :, :, HALF:HD], c_[:, :, :, 0:HALF], ALU.add)
                    if step in (0, 2):
                        link(last)
                return last

            def square_sums(j, heads, first):
                two = slice(2 * j, 2 * j + 2)
                return nc.vector.tensor_reduce(ssum[:, two, first:first + heads],
                                               sq[:, two, 0:heads * HD].rearrange("p i (g d) -> p i g d", d=HD),
                                               AX_X, ALU.add)

            def k_sums(j):
                dve.wait_ge(a_ksq, 2 * j + 2)
                square_sums(j, G, HH * G).then_inc(v_ksum, 1)

            find(3)
            link(nc.vector.tensor_single_scalar(nobody[:], best[:], 0.0, ALU.is_equal))
            link(nc.vector.scalar_tensor_tensor(out=nobody[:], in0=nobody[:], scalar=NONE, in1=row_of[:], op0=ALU.mult, op1=ALU.add))
            link(nc.vector.tensor_tensor(best[:], best[:], nobody[:], ALU.add))
            nc.vector.tensor_scalar(patch_idx[:], best[:], -BIAS, None, ALU.add).then_inc(v_patch, 1)

            dve.wait_ge(g_rot, 4)
            k_sums(0)
            for j in range(TILES // 2):
                dve.wait_ge(a_kroot, j + 1)
                if j + 1 < TILES // 2:
                    k_sums(j + 1)
                rotate(1, G, j).then_inc(v_k, 1)

            dve.wait_ge(z_misc, 2)
            link(nc.vector.tensor_scalar(lens_dyn[32:64, :], iv("lens_rb", slice(32, 64)), -1.0, float(WINDOW), ALU.mult, ALU.add))
            nc.vector.tensor_scalar(maskr[32:64, 0:WINDOW], cv("key", slice(32, 64)), lens_dyn[32:64, 0:1], MASKED,
                                    ALU.is_lt, ALU.mult).then_inc(v_dyn, 1)

            def q_sums(j):
                dve.wait_ge(a_qsq, 2 * j + 2)
                square_sums(j, HH * G, 0).then_inc(v_qsum, 1)

            q_sums(0)
            q_sums(1)
            dve.wait_ge(a_qroot, 1)
            rotate(0, HH * G, 0).then_inc(v_q, 1)

            def qbd_out(g):
                dve.wait_ge(p_qT, g + 1)
                if g >= 2:
                    dve.wait_ge(p_s, BT * (g - 1))
                if g == 0:
                    dve.wait_ge(z_misc, 4)
                for j in range(G // 2):
                    rows = slice(HD * j, HD * j + HD)
                    last = nc.vector.tensor_copy(qbd[rows, g % 2, :, j, :],
                                                 bank[2][rows, 0:HH * P].rearrange("p (n t) -> p n t", t=T))
                last.then_inc(v_qbd, 1)

            def new_keys_out(g):
                dve.wait_ge(p_kn, g + 1)
                if g >= 2:
                    dve.wait_ge(p_s, BT * (g - 1))
                first = BT * g % 8
                nc.vector.tensor_copy(ring[:, first:first + BT, STEP_W:],
                                      kn_ps.rearrange("p (b t) -> p b t", b=BT)).then_inc(v_kn, 1)

            def max_of(n):
                dve.wait_ge(p_s, n + 1)
                if n >= 4:
                    dve.wait_ge(a_exp, HH * (n - 3))
                nc.vector.tensor_reduce(negmax[:, n % 4, :], S_ps[n % 2], AX_X, ALU.max, negate=True).then_inc(v_max, 1)

            def sums_of(g):
                dve.wait_ge(a_exp, HH * BT * (g + 1))
                if g >= 2:
                    dve.wait_ge(p_ptn, g - 1)
                link(nc.vector.reciprocal(rsum[:], esum[:, g % 2, :]))
                nc.vector.tensor_tensor(rdiag[:, g % 2, :, :], free(cv("t_eye"), (0, BT * HH), (1, T)),
                                        free(rsum[:], (1, BT * HH), (0, T)), ALU.mult).then_inc(v_rdiag, 1)

            def new_probs_in(g):
                if g >= 2:
                    dve.wait_ge(p_ptn, g - 1)
                first = BT * g % 8
                nc.vector.tensor_copy(Pr_new[:, g % 2, :, :, :],
                                      Pr[:, first:first + BT, :, WINDOW:].rearrange("p n h k -> p h n k")).then_inc(v_new, 1)

            def new_probs_out(g):
                dve.wait_ge(p_ptn, g + 1)
                if g >= 2:
                    dve.wait_ge(p_o, BT * (g - 1))
                elif g == 0:
                    dve.wait_ge(z_misc, 4)
                nc.vector.tensor_copy(rsum_wide[:P // 2, g % 2, :], rsum_ps[:P // 2]).then_inc(v_rsum, 1)
                for j in range(BT // 2):
                    rows = slice(T * j, T * j + T)
                    last = nc.vector.tensor_copy(PTbd[rows, g % 2, :, j, :, :], PTn_by_head(rows))
                last.then_inc(v_ptn, 1)

            def o_out(g):
                dve.wait_ge(p_o, BT * (g + 1))
                dve.wait_ge(v_rsum, g + 1)
                dve.wait_ge(a_ptn, g + 1)
                if g >= 2:
                    dve.wait_ge(p_res, g - 1)
                nc.vector.tensor_tensor(oT[:, g % 2, :, :, :].rearrange("p h b t -> p b h t"), O_ps,
                                        rsum_wide[:, g % 2, :].rearrange("p (b h t) -> p b h t", b=BT, h=HH),
                                        ALU.mult).then_inc(v_o, 1)

            def res_out(g):
                dve.wait_ge(p_res, g + 1)
                if g >= 2:
                    dve.wait_ge(s_out[g % 2], 16 * (g // 2))
                elif g == 0:
                    dve.wait_ge(a_x3, TILES)
                nc.vector.tensor_tensor(res[:, g % 2, :], res_ps[g], x1[:, g, :], ALU.add).then_inc(v_res, 1)

            qbd_out(0)
            q_sums(2)
            q_sums(3)
            new_keys_out(0)
            for n in range(B + 6):
                g, k = divmod(n, BT)
                if n < B:
                    max_of(n)
                if k == 1 and n >= 9:
                    o_out((n - 9) // BT)
                if k == 0 and 1 <= g <= TILES:
                    sums_of(g - 1)
                    new_probs_in(g - 1)
                if k == 3 and 1 <= g <= TILES:
                    new_probs_out(g - 1)
                if k == 2 and g + 1 < TILES:
                    new_keys_out(g + 1)
                if k == 2 and g + 1 < TILES:
                    qbd_out(g + 1)
                if k == 3 and 10 <= n < B:
                    res_out((n - 11) // BT)
                j, at = n // 8 + 1, n % 8
                if j < TILES // 2 and at < 4:
                    if at == 0:
                        dve.wait_ge(a_qroot, j + 1)
                    last = rotate(0, HH * G, j, (at,))
                    if at == 3:
                        last.then_inc(v_q, 1)
            res_out(TILES - 2)
            res_out(TILES - 1)

        @block.tensor
        def _(pe):
            pe.wait_ge(s_low, 16)
            Wt_v, AT_v, Bo_v, Wp_v = lv("Wt"), lv("AT"), lv("Bo"), lv("WpT")
            for c in range(C):
                for j in range(C):
                    last = nc.tensor.matmul(AW_ps[:, c, :], Wt_v[:, j, P * c:P * c + P], AT_v[:, j, :],
                                            start=(j == 0), stop=(j == C - 1))
            last.then_inc(p_AW, 1)
            pe.wait_ge(v_look, 2)
            nc.tensor.matmul(looked_ps[:, :, 0:B], ones[:], look_all[:].rearrange("p m (r b) -> p (m r) b", b=B),
                             start=True, stop=True)
            nc.tensor.matmul(looked_ps[:, :, B:NCOL], cv("same"), look_own[:].rearrange("p m (r n) -> p (m r) n", n=TILES),
                             start=True, stop=True).then_inc(p_look, 1)
            for j in range(C):
                last = nc.tensor.matmul(C_ps, Bo_v[:, j, :], Wp_v[:, j, :], start=(j == 0), stop=(j == C - 1))
            last.then_inc(p_C, 1)
            pe.wait_ge(s_x, 16)
            pe.wait_ge(a_AW, 1)
            for h in range(2):
                for c in range(C):
                    last = nc.tensor.matmul(z_ps[h][0:ER, :], AW_sb[:, c, :], xT_sb[:, c, 512 * h:512 * h + 512],
                                            start=(c == 0), stop=(c == C - 1))
                last.then_inc(p_z, 1)
            pe.wait_ge(v_wb, C)
            pe.wait_ge(a_C, 1)
            for i in range(TILES):
                rows = slice(P * i, P * i + P)
                if i >= 3:
                    pe.wait_ge(a_x1, i - 2)
                for c in range(C):
                    nc.tensor.matmul(x1_ps[i % 3], xT_sb[:, c, rows], Wb_sb[:, c, :], start=(c == 0), stop=False)
                pe.wait_ge(v_zm, i // 4 + 1)
                nc.tensor.matmul(x1_ps[i % 3], zm[:, rows], C_sb[:], start=False, stop=True).then_inc(p_x1, 1)
                if i in (4, 5):
                    if i == 4:
                        pe.wait_ge(s_bd1, 16 * BT)
                        pe.wait_ge(g_B2, 1)
                    h = i - 4
                    for j in range(4 * h, 4 * h + 4):
                        last = nc.tensor.matmul(M_ps[h][:, j % 4, :], bd1[:, j, :], bd2[:, j, :], start=True, stop=True)
                    last.then_inc(p_M, 1)
            def mix(i):
                pe.wait_ge(v_M, i // 4 + 1)
                pe.wait_ge(a_x1, i + 1)
                if i >= 2:
                    pe.wait_ge(a_x3T, i - 1)
                elif i == 0:
                    pe.wait_ge(v_zm, 2)
                for c in range(C):
                    last = nc.tensor.matmul(x3T_ps[i % 2][:, c, :], x1[:, i, P * c:P * c + P], M_sb[:, i, :],
                                            start=True, stop=True)
                last.then_inc(p_x3T, 1)

            pe.wait_ge(s_qkvw, 16)
            mix(0)
            for i in range(TILES):
                if i + 1 < TILES:
                    mix(i + 1)
                pe.wait_ge(a_x3T, i + 1)
                if i >= 3:
                    pe.wait_ge(a_kv, i - 2)
                elif i == 0:
                    pe.wait_ge(a_x1, TILES)
                for c in range(C):
                    last = nc.tensor.matmul(kv_ps[i % 3], x3T[:, i, c, :], Wqkv_sb[:, c, QW:],
                                            start=(c == 0), stop=(c == C - 1))
                last.then_inc(p_kv, 1)
            for i in range(TILES):
                if i >= 3:
                    pe.wait_ge(a_qraw, i - 2)
                elif i == 0:
                    pe.wait_ge(v_M, 2)
                for c in range(C):
                    last = nc.tensor.matmul(q_ps[i % 3], x3T[:, i, c, :], Wqkv_sb[:, c, 0:QW],
                                            start=(c == 0), stop=(c == C - 1))
                last.then_inc(p_qraw, 1)
                if i >= 2:
                    pe.wait_ge(a_x3, i - 1)
                elif i == 0:
                    pe.wait_ge(a_x3T, TILES)
                nc.tensor.matmul(x3_ps[i % 2], M_sb[:, i, :], x1[:, i, :], start=True, stop=True).then_inc(p_x3, 1)

            def queries_in(g):
                pe.wait_ge(v_q, g // 2 + 1)
                if g >= 1:
                    pe.wait_ge(a_qbd, g)
                    pe.wait_ge(v_qbd, g)
                else:
                    pe.wait_ge(a_qraw, TILES)
                for h in range(HH):
                    last = nc.tensor.transpose(qT_ps[:, h, :], qkv[:, g, KW * h:KW * h + KW], cv("ident"))
                last.then_inc(p_qT, 1)

            def new_keys_in(g):
                pe.wait_ge(s_own[g], 16)
                if g >= 1:
                    pe.wait_ge(v_kn, g)
                    if g >= 4:
                        pe.wait_ge(v_res, g - 3)
                else:
                    pe.wait_ge(a_kv, TILES)
                nc.tensor.transpose(kn_ps, qkv[:, g, QW:QW + KW], cv("ident")).then_inc(p_kn, 1)

            def step_in(m):
                if m >= 0:
                    pe.wait_ge(a_step, m + 1)
                elif m == -2:
                    pe.wait_ge(a_x3, TILES)
                ps = step_ps[m % 2]
                if m + 2 < B:
                    pe.wait_ge(s_patch[m + 2], 16)
                    last = nc.tensor.transpose(ps[:, HH * WINDOW:], hist[:, m + 2, 0:KW], cv("ident"))
                if m >= 2:
                    pe.wait_ge(a_exp, HH * (m - 1))
                    for h in range(HH):
                        last = nc.tensor.transpose(ps[:, WINDOW * h:WINDOW * h + WINDOW], Pr[:, (m - 2) % 8, h, 0:WINDOW],
                                                   cv("ident"))
                last.then_inc(p_step, 1)

            def scores(n):
                g, j = divmod(n, BT)
                pe.wait_ge(a_step, n + 1)
                if j == 0:
                    pe.wait_ge(v_kn, g + 1)
                    pe.wait_ge(v_qbd, g + 1)
                    pe.wait_ge(a_qbd, g + 1)
                if n == 0:
                    pe.wait_ge(s_mask, 32)
                    pe.wait_ge(v_dyn, 1)
                if n >= 2:
                    pe.wait_ge(a_exp, HH * (n - 1))
                nc.tensor.matmul(S_ps[n % 2], sel_sb[:, n, :], free(maskr[:], (0, HH), (1, KEYS)), start=True, stop=False)
                for h in range(HH):
                    last = nc.tensor.matmul(S_ps[n % 2][:, h, :], qbd[:, g % 2, BT * h + j, :, :].rearrange("p g t -> p (g t)"),
                                            ring[:, n % 8, HH * WINDOW:], start=False, stop=(h == HH - 1))
                last.then_inc(p_s, 1)

            def new_probs_in(g):
                if g >= 1:
                    pe.wait_ge(a_ptn, g)
                    pe.wait_ge(v_ptn, g)
                else:
                    pe.wait_ge(a_kv, TILES)
                pe.wait_ge(v_rdiag, g + 1)
                pe.wait_ge(v_new, g + 1)
                for h in range(HH):
                    nc.tensor.transpose(PTn_ps[:, h, :], Pr_new[:, g % 2, h, :, :].rearrange("p n k -> p (n k)"), cv("ident"))
                nc.tensor.matmul(rsum_ps, cv("group"), rdiag[:, g % 2, :, :].rearrange("p n t -> p (n t)"),
                                 start=True, stop=True).then_inc(p_ptn, 1)

            def new_values(g):
                pe.wait_ge(a_ptn, g + 1)
                pe.wait_ge(v_ptn, g + 1)
                for k in range(G):
                    last = nc.tensor.matmul(bank[6][HD * k:HD * k + HD, 0:BT * HH * T],
                                            qkv[:, g, QW + KW + HD * k:QW + KW + HD * k + HD],
                                            PTbd[:, g % 2, k, :, :, :].rearrange("p b h t -> p (b h t)"), start=False, stop=True)
                return last

            def values(n):
                g, j = divmod(n, BT)
                pe.wait_ge(a_step, n + 5)
                if j == 0 and g >= 1:
                    pe.wait_ge(v_o, g)
                for k in range(G):
                    rows = slice(HD * k, HD * k + HD)
                    cols = slice(T * k, T * k + T)
                    last = nc.tensor.matmul(O_ps[rows, j], hist[:, n, KW + HD * k:KW + HD * k + HD],
                                            free(ring[:, (n + 4) % 8, cols], (WINDOW, HH), (1, T)),
                                            start=(j == 0), stop=False)
                if j == BT - 1:
                    last = new_values(g)
                last.then_inc(p_o, 1)

            def rows_out(g):
                if g == TILES - 1:
                    pe.wait_ge(a_exp, HH * B)
                else:
                    if g >= 1:
                        pe.wait_ge(v_res, g)
                    pe.wait_ge(v_kn, min(g + 4, TILES))
                pe.wait_ge(v_o, g + 1)
                for h in range(HH):
                    last = nc.tensor.matmul(res_ps[g], oT[:, g % 2, h, :, :].rearrange("p b t -> p (b t)"), Wo_sb[:, h, :],
                                            start=(h == 0), stop=(h == HH - 1))
                last.then_inc(p_res, 1)

            queries_in(0)
            new_keys_in(0)
            step_in(-2)
            step_in(-1)
            pe.wait_ge(s_wo, 16)
            for n in range(B + 6):
                g, k = divmod(n, BT)
                if n < B:
                    scores(n)
                if k == 2 and g + 1 < TILES:
                    new_keys_in(g + 1)
                if k == 2 and 1 <= g <= TILES:
                    new_probs_in(g - 1)
                if n < B + 2:
                    step_in(n)
                if k == 1 and g + 1 < TILES:
                    queries_in(g + 1)
                if 6 <= n < B + 6:
                    values(n - 6)
                if k == 3 and 10 <= n < B:
                    rows_out((n - 10) // BT)
            rows_out(TILES - 2)
            rows_out(TILES - 1)


def kernel(**inputs):
    import concourse.bacc as bacc
    from concourse.bass_utils import run_bass_kernel_spmd

    a = {k: np.asarray(v) for k, v in inputs.items()}
    lens = a["itok_B_37_3939"]

    def heads_last(w):
        return w.reshape(G, HH, HD, D).transpose(3, 1, 0, 2).reshape(D, QW)

    def by_position(blocks):
        return blocks.transpose(0, 2, 1, 3).reshape(-1, KW)

    def over_partitions(w):
        return w.reshape(C, P, -1).transpose(1, 0, 2).reshape(P, -1)

    def every(v):
        return np.tile(v[None], (P, 1))

    band, select = mask_constants()
    per_batch = [np.tile(v.reshape(B, -1), (P // B, 1)) for v in (
        lens, a["itok_B_0_7"], a["itok_B_1_198"], a["itok_Bx257_0_4111"])]
    arrays = {
        "ints": np.concatenate([every(lens), np.repeat(lens.reshape(TILES, BT).T, T, 0), *per_batch[:3],
                                every(a["itok_B_0_3"]), per_batch[3]], axis=1),
        "const": np.concatenate([constants()[:, :CONST["q_scale"][0]], every(a["L3_cond_q_norm_scale"]),
                                 every(a["L3_cond_k_norm_scale"]),
                                 np.tile(np.repeat(a["L0_cond_scaling"], R), P // ER)[:, None]], axis=1),
        "low": np.concatenate([over_partitions(w) for w in (
            a["L0_cond_Wt"], a["L0_cond_A"].reshape(ER, D).T,
            a["L0_cond_B_w"].transpose(1, 0, 2).reshape(D, ER), a["L0_cond_Wp"].T)], axis=1),
        "xT": over_partitions(a["x"].reshape(TOK, D).T),
        "WbT": over_partitions(a["L0_cond_W_base"].T),
        "W1T": a["L1_cond_weights"].transpose(0, 2, 1).reshape(-1, T * T),
        "W2": a["L2_cond_weights"].reshape(-1, T * T),
        "WqkvT": over_partitions(np.concatenate(
            [heads_last(a["L3_cond_Wq"]), a["L3_cond_Wk"].T, a["L3_cond_Wv"].T], axis=1)),
        "WoT": over_partitions(a["L3_cond_Wo"].reshape(D, G, HH, HD).transpose(2, 1, 3, 0).reshape(D, D)),
        "cache": np.concatenate([by_position(a["L3_cond_k_blocks"]), by_position(a["L3_cond_v_blocks"])], axis=1),
        "band": band,
        "select": select,
    }
    arrays = {k: np.ascontiguousarray(v) for k, v in arrays.items()}
    nc = bacc.Bacc("TRN2", target_bir_lowering=False, num_devices=1)
    args = [nc.dram_tensor(k, v.shape, mybir.dt.from_np(v.dtype), kind="ExternalInput").ap() for k, v in arrays.items()]
    for name, shape in (("new_rows", [TOK, 2 * KW]), ("w1_rows", [B, T * T]), ("w2_rows", [B, T * T])):
        args.append(nc.dram_tensor(name, shape, F32, kind="Internal").ap())
    args.append(nc.dram_tensor("out", [TOK, D], F32, kind="ExternalOutput").ap())
    cond_resid_kernel(nc, *args)
    got = run_bass_kernel_spmd(nc, [arrays], core_ids=[0])
    return got.results[0]["out"].reshape(B, T, D)
```
